# Optimizing a Trainium2 kernel written in Bass

```python
import numpy as np
import jax
import jax.numpy as jnp

def _softmax(x, axis=-1):
    return jax.nn.softmax(x, axis=axis)

def _gelu(x):
    return jax.nn.gelu(x, approximate=True)

def _silu(x):
    return jax.nn.silu(x)

def _sigmoid(x):
    return jax.nn.sigmoid(x)

def _layernorm(x, axis=-1, eps=1e-05):
    m = jnp.mean(x, axis=axis, keepdims=True)
    v = jnp.var(x, axis=axis, keepdims=True)
    return (x - m) / jnp.sqrt(v + eps)

def _scatter_add(tgt, idx, src, axis=0):
    return tgt.at[idx].add(src)

def _segment_sum(src, seg, n):
    return jax.ops.segment_sum(src, seg, n)
kernel_name = 'mk_adaln_attn_ffn_d1_seqx_r8_e28fe4'

def setup_inputs(seed: int=0):
    np.random.seed(seed)
    _w = jnp.asarray

    def _rec_inputs():
        import jax
        import jax.numpy as jnp
        _rk = jax.random.key(seed)
        x = -0.000125 + 0.9999 * jax.random.normal(jax.random.fold_in(_rk, 1), (8, 128, 512), jnp.float32)
        _lenS = 128 - jax.random.randint(jax.random.fold_in(_rk, 7), (8,), 0, max(1, 128 // 4) + 1, jnp.int32)
        _lenS2 = 128 - jax.random.randint(jax.random.fold_in(_rk, 8), (8,), 0, max(1, 128 // 4) + 1, jnp.int32)
        itok_B_3_7 = jax.random.randint(jax.random.fold_in(_rk, 11), (8,), 3, 8, jnp.int32)
        itok_B_0_23 = jax.random.randint(jax.random.fold_in(_rk, 12), (8,), 0, 24, jnp.int32)
        return (x, itok_B_3_7, itok_B_0_23)
    x, itok_B_3_7, itok_B_0_23 = _rec_inputs()

    def _L0_cond_setup():
        import jax, jax.numpy as jnp
        import numpy as np
        MAX_LORAS, OUT, IN = (8, 512, 512)
        B, S = (4, 256)
        key = jax.random.key(seed)
        k1, k2, k3 = jax.random.split(key, 3)
        x = jax.random.normal(k1, (B, S, IN), dtype=jnp.float32)
        weight = jax.random.normal(k2, (MAX_LORAS, OUT, IN), dtype=jnp.float32) * 0.02
        adapter_ids = jax.random.randint(k3, (B,), 0, MAX_LORAS, dtype=jnp.int32)
        return {'x': x, 'weight': weight, 'adapter_ids': adapter_ids}
    _L0_cond_all = _L0_cond_setup()
    _L0_cond_in = {k: v for k, v in _L0_cond_all.items() if k in ('weight',)}
    del _L0_cond_all

    def _L0_attn_setup():
        import jax, jax.numpy as jnp
        import numpy as np
        import math
        HIDDEN = 512
        N_HEADS = 32
        N_KV_HEADS = 8
        HEAD_DIM = HIDDEN // N_HEADS
        GROUPS = N_HEADS // N_KV_HEADS
        ROPE_THETA = 10000.0
        TOKEN_BUDGET = 128
        INIT_BUDGET = 128
        RECENT_BUDGET = 128
        CHUNK = 16
        B, S = (1, 256)

        def _rotate_half(x):
            x1, x2 = jnp.split(x, 2, axis=-1)
            return jnp.concatenate([-x2, x1], axis=-1)

        def _rope(seq_len, dtype):
            inv_freq = 1.0 / ROPE_THETA ** (jnp.arange(0, HEAD_DIM, 2, dtype=jnp.float32) / HEAD_DIM)
            freqs = jnp.arange(seq_len, dtype=jnp.float32)[:, None] * inv_freq[None, :]
            emb = jnp.concatenate([freqs, freqs], axis=-1)
            return (jnp.cos(emb).astype(dtype), jnp.sin(emb).astype(dtype))
        key = jax.random.key(seed)
        ks = jax.random.split(key, 5)
        sc = 0.02
        return {'hidden_states': jax.random.normal(ks[0], (B, S, HIDDEN), dtype=jnp.float32), 'wq': jax.random.normal(ks[1], (N_HEADS * HEAD_DIM, HIDDEN), dtype=jnp.float32) * sc, 'wk': jax.random.normal(ks[2], (N_KV_HEADS * HEAD_DIM, HIDDEN), dtype=jnp.float32) * sc, 'wv': jax.random.normal(ks[3], (N_KV_HEADS * HEAD_DIM, HIDDEN), dtype=jnp.float32) * sc, 'wo': jax.random.normal(ks[4], (HIDDEN, N_HEADS * HEAD_DIM), dtype=jnp.float32) * sc}
    _L0_attn_all = _L0_attn_setup()
    _L0_attn_in = {k: v for k, v in _L0_attn_all.items() if k in ('wq', 'wk', 'wv', 'wo')}
    del _L0_attn_all

    def _L0_cond2_setup():
        import jax, jax.numpy as jnp
        import numpy as np
        R = 16
        ALPHA = 32
        SCALING = ALPHA / R
        SLOTS = 32
        IN_F = 512
        OUT_F = 512
        B, T = (8, 128)
        key = jax.random.key(seed)
        k1, k2, k3, k4, k5, k6 = jax.random.split(key, 6)
        x = jax.random.normal(k1, (B, T, IN_F), dtype=jnp.float32)
        adapter_mapping = jax.random.randint(k2, (B,), 0, SLOTS, dtype=jnp.int32)
        W = jax.random.normal(k3, (OUT_F, IN_F), dtype=jnp.float32) * 0.02
        b = jax.random.normal(k4, (OUT_F,), dtype=jnp.float32) * 0.02
        lora_As = jax.random.normal(k5, (SLOTS, IN_F, R), dtype=jnp.float32) * 0.02
        lora_Bs = jax.random.normal(k6, (SLOTS, R, OUT_F), dtype=jnp.float32) * 0.02
        return {'x': x, 'adapter_mapping': adapter_mapping, 'W': W, 'b': b, 'lora_As': lora_As, 'lora_Bs': lora_Bs}
    _L0_cond2_all = _L0_cond2_setup()
    _L0_cond2_in = {k: v for k, v in _L0_cond2_all.items() if k in ('W', 'b', 'lora_As', 'lora_Bs')}
    del _L0_cond2_all

    def _L0_ffn_setup():
        import jax, jax.numpy as jnp
        import numpy as np
        H = 512
        I = 1376
        R = 32
        NLEV = 16
        Q_ZERO = 7.5
        Q_STEP = 0.005
        LR_SCALE = 0.02

        def _qlinear(x, q, scale, A, Bm):
            w = (q.astype(jnp.float32) - Q_ZERO) * (scale * Q_STEP)[:, None]
            y = jnp.einsum('bsh,oh->bso', x, w)
            return y + LR_SCALE * (x @ A @ Bm)
        key = jax.random.key(seed)
        ks = jax.random.split(key, 13)
        B, S = (2, 256)
        inp = {'x': jax.random.normal(ks[0], (B, S, H), jnp.float32), 'gate_q': jax.random.randint(ks[1], (I, H), 0, NLEV, jnp.int32), 'gate_scale': jax.random.uniform(ks[2], (I,), jnp.float32), 'gate_A': jax.random.normal(ks[3], (H, R), jnp.float32), 'gate_B': jax.random.normal(ks[4], (R, I), jnp.float32), 'up_q': jax.random.randint(ks[5], (I, H), 0, NLEV, jnp.int32), 'up_scale': jax.random.uniform(ks[6], (I,), jnp.float32), 'up_A': jax.random.normal(ks[7], (H, R), jnp.float32), 'up_B': jax.random.normal(ks[8], (R, I), jnp.float32), 'down_q': jax.random.randint(ks[9], (H, I), 0, NLEV, jnp.int32), 'down_scale': jax.random.uniform(ks[10], (H,), jnp.float32), 'down_A': jax.random.normal(ks[11], (I, R), jnp.float32), 'down_B': jax.random.normal(ks[12], (R, H), jnp.float32)}
        return inp
    _L0_ffn_all = _L0_ffn_setup()
    _L0_ffn_in = {k: v for k, v in _L0_ffn_all.items() if k in ('gate_q', 'gate_scale', 'gate_A', 'gate_B', 'up_q', 'up_scale', 'up_A', 'up_B', 'down_q', 'down_scale', 'down_A', 'down_B')}
    del _L0_ffn_all
    return {'x': x, 'itok_B_3_7': itok_B_3_7, 'itok_B_0_23': itok_B_0_23, 'L0_cond_weight': _L0_cond_in['weight'], 'L0_attn_wq': _L0_attn_in['wq'], 'L0_attn_wk': _L0_attn_in['wk'], 'L0_attn_wv': _L0_attn_in['wv'], 'L0_attn_wo': _L0_attn_in['wo'], 'L0_cond2_W': _L0_cond2_in['W'], 'L0_cond2_b': _L0_cond2_in['b'], 'L0_cond2_lora_As': _L0_cond2_in['lora_As'], 'L0_cond2_lora_Bs': _L0_cond2_in['lora_Bs'], 'L0_ffn_gate_q': _L0_ffn_in['gate_q'], 'L0_ffn_gate_scale': _L0_ffn_in['gate_scale'], 'L0_ffn_gate_A': _L0_ffn_in['gate_A'], 'L0_ffn_gate_B': _L0_ffn_in['gate_B'], 'L0_ffn_up_q': _L0_ffn_in['up_q'], 'L0_ffn_up_scale': _L0_ffn_in['up_scale'], 'L0_ffn_up_A': _L0_ffn_in['up_A'], 'L0_ffn_up_B': _L0_ffn_in['up_B'], 'L0_ffn_down_q': _L0_ffn_in['down_q'], 'L0_ffn_down_scale': _L0_ffn_in['down_scale'], 'L0_ffn_down_A': _L0_ffn_in['down_A'], 'L0_ffn_down_B': _L0_ffn_in['down_B']}

def reference(x, itok_B_3_7, itok_B_0_23, L0_cond_weight, L0_attn_wq, L0_attn_wk, L0_attn_wv, L0_attn_wo, L0_cond2_W, L0_cond2_b, L0_cond2_lora_As, L0_cond2_lora_Bs, L0_ffn_gate_q, L0_ffn_gate_scale, L0_ffn_gate_A, L0_ffn_gate_B, L0_ffn_up_q, L0_ffn_up_scale, L0_ffn_up_A, L0_ffn_up_B, L0_ffn_down_q, L0_ffn_down_scale, L0_ffn_down_A, L0_ffn_down_B):
    import jax
    import jax.numpy as jnp

    def _L0_cond_ref(x, weight, adapter_ids):
        import jax, jax.numpy as jnp
        import numpy as np
        MAX_LORAS, OUT, IN = (8, 512, 512)
        B, S = (4, 256)
        w = weight[adapter_ids]
        return jnp.einsum('bsi,boi->bso', x, w)

    def _L0_attn_ref(hidden_states, wq, wk, wv, wo):
        import jax, jax.numpy as jnp
        import numpy as np
        import math
        HIDDEN = 512
        N_HEADS = 32
        N_KV_HEADS = 8
        HEAD_DIM = HIDDEN // N_HEADS
        GROUPS = N_HEADS // N_KV_HEADS
        ROPE_THETA = 10000.0
        TOKEN_BUDGET = 128
        INIT_BUDGET = 128
        RECENT_BUDGET = 128
        CHUNK = 16
        B, S = (1, 256)

        def _rotate_half(x):
            x1, x2 = jnp.split(x, 2, axis=-1)
            return jnp.concatenate([-x2, x1], axis=-1)

        def _rope(seq_len, dtype):
            inv_freq = 1.0 / ROPE_THETA ** (jnp.arange(0, HEAD_DIM, 2, dtype=jnp.float32) / HEAD_DIM)
            freqs = jnp.arange(seq_len, dtype=jnp.float32)[:, None] * inv_freq[None, :]
            emb = jnp.concatenate([freqs, freqs], axis=-1)
            return (jnp.cos(emb).astype(dtype), jnp.sin(emb).astype(dtype))
        b, s, _ = hidden_states.shape
        dtype = hidden_states.dtype
        NEG = jnp.finfo(dtype).min
        q = (hidden_states @ wq.T).reshape(b, s, N_HEADS, HEAD_DIM).transpose(0, 2, 1, 3)
        k = (hidden_states @ wk.T).reshape(b, s, N_KV_HEADS, HEAD_DIM).transpose(0, 2, 1, 3)
        v = (hidden_states @ wv.T).reshape(b, s, N_KV_HEADS, HEAD_DIM).transpose(0, 2, 1, 3)
        cos, sin = _rope(s, dtype)
        q = q * cos[None, None] + _rotate_half(q) * sin[None, None]
        k = k * cos[None, None] + _rotate_half(k) * sin[None, None]
        k = jnp.repeat(k, GROUPS, axis=1)
        v = jnp.repeat(v, GROUPS, axis=1)
        scores = jnp.einsum('bhqd,bhkd->bhqk', q, k) / math.sqrt(HEAD_DIM)
        q_pos = jnp.arange(s)[:, None]
        k_pos = jnp.arange(s)[None, :]
        causal = k_pos <= q_pos
        masked = jnp.where(causal[None, None], scores, NEG)
        pad = -s % CHUNK
        padded = jnp.pad(masked, ((0, 0), (0, 0), (0, 0), (0, pad)), constant_values=NEG)
        n_chunks = (s + pad) // CHUNK
        chunk_max = padded.reshape(b, N_HEADS, s, n_chunks, CHUNK).max(axis=-1)
        k_top = min(max(3, TOKEN_BUDGET // CHUNK), n_chunks)
        _, topk_idx = jax.lax.top_k(chunk_max, k_top)
        chunk_mask = jnp.any(topk_idx[..., None] == jnp.arange(n_chunks), axis=-2)
        tok_mask = jnp.repeat(chunk_mask, CHUNK, axis=-1)[..., :s]
        init_mask = k_pos < INIT_BUDGET
        recent_mask = k_pos > q_pos - RECENT_BUDGET
        allowed = causal[None, None] & (tok_mask | init_mask[None, None] | recent_mask[None, None])
        final = jnp.where(allowed, scores, NEG)
        attn = jax.nn.softmax(final, axis=-1)
        out = jnp.einsum('bhqk,bhkd->bhqd', attn, v)
        out = out.transpose(0, 2, 1, 3).reshape(b, s, N_HEADS * HEAD_DIM)
        return out @ wo.T

    def _L0_cond2_ref(x, adapter_mapping, W, b, lora_As, lora_Bs):
        import jax, jax.numpy as jnp
        import numpy as np
        R = 16
        ALPHA = 32
        SCALING = ALPHA / R
        SLOTS = 32
        IN_F = 512
        OUT_F = 512
        B, T = (8, 128)
        base_out = jnp.einsum('bti,oi->bto', x, W) + b
        A = lora_As[adapter_mapping]
        Bm = lora_Bs[adapter_mapping]
        lora_h = jnp.einsum('bti,bir->btr', x, A)
        lora_out = jnp.einsum('btr,bro->bto', lora_h, Bm)
        return base_out + lora_out * SCALING

    def _L0_ffn_ref(x, gate_q, gate_scale, gate_A, gate_B, up_q, up_scale, up_A, up_B, down_q, down_scale, down_A, down_B):
        import jax, jax.numpy as jnp
        import numpy as np
        H = 512
        I = 1376
        R = 32
        NLEV = 16
        Q_ZERO = 7.5
        Q_STEP = 0.005
        LR_SCALE = 0.02

        def _qlinear(x, q, scale, A, Bm):
            w = (q.astype(jnp.float32) - Q_ZERO) * (scale * Q_STEP)[:, None]
            y = jnp.einsum('bsh,oh->bso', x, w)
            return y + LR_SCALE * (x @ A @ Bm)
        g = _qlinear(x, gate_q, gate_scale, gate_A, gate_B)
        u = _qlinear(x, up_q, up_scale, up_A, up_B)
        h = jax.nn.silu(g) * u
        return _qlinear(h, down_q, down_scale, down_A, down_B)
    x = x + _L0_attn_ref(_L0_cond_ref(x, L0_cond_weight, itok_B_3_7), L0_attn_wq, L0_attn_wk, L0_attn_wv, L0_attn_wo)
    x = x + _L0_ffn_ref(_L0_cond2_ref(x, itok_B_0_23, L0_cond2_W, L0_cond2_b, L0_cond2_lora_As, L0_cond2_lora_Bs), L0_ffn_gate_q, L0_ffn_gate_scale, L0_ffn_gate_A, L0_ffn_gate_B, L0_ffn_up_q, L0_ffn_up_scale, L0_ffn_up_A, L0_ffn_up_B, L0_ffn_down_q, L0_ffn_down_scale, L0_ffn_down_A, L0_ffn_down_B)
    return x

_drawn_inputs = setup_inputs


def setup_inputs(seed=0):
    import zlib

    import numpy as np

    out = dict(_drawn_inputs(seed))
    spreads = {}
    factors = {'L0_attn_wq': 8.0, 'L0_attn_wk': 8.0}
    for name, (base, spread) in spreads.items():
        noise = np.random.default_rng([zlib.crc32(name.encode()), seed]).standard_normal(out[name].shape)
        drawn = base * np.exp(spread * noise) if base else spread * noise
        out[name] = jnp.asarray(drawn.astype(out[name].dtype))
    for name, factor in factors.items():
        out[name] = (out[name] * factor).astype(out[name].dtype)
    return out
```

```python
from contextlib import ExitStack

import concourse.bass as bass
from concourse import mybir

ALU = mybir.AluOpType
ACT = mybir.ActivationFunctionType
AX_X = mybir.AxisListType.X
F32 = mybir.dt.float32
F32R = mybir.dt.float32r
BF16 = mybir.dt.bfloat16
I32 = mybir.dt.int32

P = 128
H = 512
KB = H // P
B, S = 8, 128
HALVES = 2
NB = B // HALVES
T = NB * S
NH, NKV, HD = 32, 8, 16
GROUPS = NH // NKV
PAIRS = NKV // 2
QK_SCALE = HD ** -0.5
ADAPTERS, SLOTS, R2 = 8, 32, 16
R = 32
I_TILES = 11
IP = I_TILES * P
PROJ = 7
Q_ZERO, Q_STEP, LR_SCALE, LORA_SCALE = 7.5, 0.005, 0.02, 2.0
D_CHUNKS = (I_TILES + 1) // 2
W_CHUNKS = I_TILES + D_CHUNKS
ST_ORDER = [0, 2, 4, 6, 1, 3, 5, 7]
MASKED = -1e30


def adaln_attn_ffn(nc, xT, ids, cond_w, proj_w, wo_w, c2_w, c2_b, c2_A, c2_B, gu_q, dn_q, scales,
                   gA, uA, gB, uB, dA, dB, rope_tab, causal, eye, key_rows, head_cols, out):
    with ExitStack() as ctx:
        def sb(name, shape, dt):
            return ctx.enter_context(nc.sbuf_tensor(name, shape, dt))

        def sem(name):
            return ctx.enter_context(nc.semaphore(name))

        bank = [ctx.enter_context(nc.psum_tensor(f"bank{k}", [P, T], F32)) for k in range(8)]

        projw = sb("projw", [P, 2, KB, PROJ * P], F32R)
        wow = sb("wow", [P, 2, KB, H], F32R)
        guA = sb("guA", [P, 2, 2, KB, P], F32R)
        guB = sb("guB", [P, 2, IP], F32R)
        dnA = sb("dnA", [P, I_TILES, 4, R], F32R)
        dnB = sb("dnB", [P, 2, H], F32R)
        headsel = sb("headsel", [NH, NKV, P], F32R)
        rope = sb("rope", [P, 2, S], F32)
        maskq = sb("maskq", [P, NB * S], BF16)
        eyef = sb("eyef", [P, P], F32)
        eyeb = sb("eyeb", [P, P], BF16)
        keyrow = sb("keyrow", [P, 4], F32)
        headcol = sb("headcol", [NH, GROUPS], F32)
        headrow = sb("headrow", [NH, NKV], F32)
        ones2 = sb("ones2", [P, 2, 32], F32)
        scale = sb("scale", [P, 2 * I_TILES + KB], F32)
        bias2 = sb("bias2", [P, KB], F32)
        ids_sb = sb("ids_sb", [1, 2 * B], I32)
        xres = sb("xres", [P, KB, T], F32)
        stage = sb("stage", [P, 4, 1024], F32)
        wf = sb("wf", [P, 2, 1024], F32R)
        vpad = sb("vpad", [P, NB, NKV, 32], F32)
        slots = sb("slots", [P, 8, T], F32)
        nrm = sb("nrm", [P, 2, T], F32)
        shift = sb("shift", [NH, GROUPS, S], F32R)
        mx = sb("mx", [P, 2, NKV, GROUPS], F32)
        loraA = sb("loraA", [P, NB, KB, R2], F32)
        loraB = sb("loraB", [P, H], F32)
        lorah = sb("lorah", [P, T], F32)
        xc = sb("xc", [P, 2, KB, T], F32R)
        with nc.sbuf_tensor("raw", [P, 10336], F32) as raw:
            pass
        arena = sb("arena", [P, 3 * 4096], F32R)

        r_proj = raw[:, 0:3584].rearrange("p (k n) -> p k n", k=KB)
        r_wo = raw[:, 3584:5632].rearrange("p (k n) -> p k n", k=KB)
        r_guA = raw[:, 5632:6656].rearrange("p (w k n) -> p w k n", w=2, k=KB)
        r_guB = raw[:, 6656:9472].rearrange("p (w n) -> p w n", w=2)
        r_dnA = raw[:, 9472:9824].rearrange("p (k n) -> p k n", n=R)
        r_dnB = raw[:, 9824:10336]

        att = xc
        qq = arena[:, 0:4096].rearrange("p (t j n) -> p t j n", t=2, j=GROUPS)
        x1 = arena[:, 0:4096].rearrange("p (a k n) -> p a k n", a=2, k=KB)
        km = arena[:, 4096:12288].rearrange("p (a g n) -> p a g n", a=2, g=NKV)
        xb = arena[:, 4096:8192].rearrange("p (a k n) -> p a k n", a=2, k=KB)
        w2 = arena[:, 8192:12288].rearrange("p (a k n) -> p a k n", a=2, k=KB)
        z = arena[:, 11264:12288].rearrange("p (w n) -> p w n", w=2)
        xcf = xc[:, :, :, :].rearrange("p a k n -> p (a k n)")

        def hid(n, part):
            if n < 4:
                return xcf[:, 1024 * n + 512 * part:1024 * n + 512 * part + 512]
            at = (1024 * (n - 4) if n < 8 else 8192 + 1024 * (n - 8)) + 512 * part
            return arena[:, at:at + 512]

        def f(ap):
            return ap.bitcast(F32)

        def wi(m):
            return (m + 2) % 4

        wi_uses = [len([m for m in range(W_CHUNKS) if wi(m) == s]) for s in range(4)]

        s_ids = sem("s_ids")
        s_const = sem("s_const")
        s_raw = [sem(f"s_raw{k}") for k in range(5)]
        s_x = sem("s_x")
        s_wc = [sem(f"s_wc{k}") for k in range(2)]
        s_w2raw = sem("s_w2raw")
        s_la = sem("s_la")
        s_lb = sem("s_lb")
        s_wi = [sem(f"s_wi{k}") for k in range(4)]
        s_out = sem("s_out")
        s_zeros = sem("s_zeros")
        s_init = sem("s_init")
        s_gate_sp = sem("s_gate_sp")
        s_gate_dve = sem("s_gate_dve")
        s_gate_pool = sem("s_gate_pool")
        s_headrow = sem("s_headrow")
        s_hi0 = sem("s_hi0")
        s_split = sem("s_split")
        s_condb = sem("s_condb")
        s_cond = sem("s_cond")
        s_xchi = sem("s_xchi")
        s_xclo = sem("s_xclo")
        s_proj = sem("s_proj")
        s_sw = sem("s_sw")
        s_cos = sem("s_cos")
        s_sin = sem("s_sin")
        s_rope = sem("s_rope")
        s_kmhi = sem("s_kmhi")
        s_kmlo = sem("s_kmlo")
        s_qhi = sem("s_qhi")
        s_qlo = sem("s_qlo")
        s_vT = sem("s_vT")
        s_vtr = sem("s_vtr")
        s_v = sem("s_v")
        s_S = sem("s_S")
        s_max = sem("s_max")
        s_mT = sem("s_mT")
        s_shift = sem("s_shift")
        s_ST = sem("s_ST")
        s_exp = sem("s_exp")
        s_p = sem("s_p")
        s_pused = sem("s_pused")
        s_rec = sem("s_rec")
        s_on = sem("s_on")
        s_ahi = sem("s_ahi")
        s_alo = sem("s_alo")
        s_wo = sem("s_wo")
        s_w2hi = sem("s_w2hi")
        s_w2lo = sem("s_w2lo")
        s_x1 = sem("s_x1")
        s_x1hi = sem("s_x1hi")
        s_x1lo = sem("s_x1lo")
        s_lh = sem("s_lh")
        s_lhs = sem("s_lhs")
        s_c2 = sem("s_c2")
        s_xbhi = sem("s_xbhi")
        s_xblo = sem("s_xblo")
        s_zp = sem("s_zp")
        s_zhi = sem("s_zhi")
        s_z = sem("s_z")
        s_wf = sem("s_wf")
        s_gu = sem("s_gu")
        s_tgu = sem("s_tgu")
        s_g = sem("s_g")
        s_u = sem("s_u")
        s_th = sem("s_th")
        s_h1 = sem("s_h1")
        s_h = sem("s_h")
        s_hhi = sem("s_hhi")
        s_hlo = sem("s_hlo")
        s_dn = sem("s_dn")
        s_dl = sem("s_dl")
        s_r1 = sem("s_r1")
        s_y = sem("s_y")

        block = ctx.enter_context(nc.Block())

        @block.sync
        def _(sp):
            sp.dma_start(ids_sb[:, :], ids).then_inc(s_ids, 16)
            sp.wait_ge(s_ids, 16)
            with sp.Fori(0, HALVES) as i:
                for b in range(NB):
                    if b == 1:
                        sp.dma_start(xres[:, :, :],
                                     xT[bass.ds(i, 1)].rearrange("a p k n -> p (a k) n")).then_inc(s_x, 16)
                    if b >= 2:
                        sp.wait_ge(s_condb, i * (NB - 1) + b - 1)
                    a = sp.value_load(ids_sb[0:1, bass.ds(i * NB + b, 1)], min_val=0, max_val=ADAPTERS - 1)
                    sp.dma_start(stage[:, 2 * (b % 2):2 * (b % 2) + 2, :].rearrange("p a n -> p (a n)"),
                                 cond_w[bass.ds(a, 1)].rearrange("a p n -> p (a n)")).then_inc(s_wc[b % 2], 16)
                sp.wait_ge(s_condb, i * (NB - 1) + 3)
                sp.dma_start(stage[:, 0:2, :].rearrange("p a n -> p (a n)"), c2_w).then_inc(s_w2raw, 16)
                for b in range(NB):
                    if b == 0:
                        sp.wait_ge(s_zeros, 4)
                    a = sp.value_load(ids_sb[0:1, bass.ds(i * NB + (B + b), 1)], min_val=0, max_val=SLOTS - 1)
                    sp.dma_start(loraA[:, b, :, :].rearrange("p k r -> p (k r)"),
                                 c2_A[bass.ds(a, 1)].rearrange("a p n -> p (a n)")).then_inc(s_la, 16)
                    sp.dma_start(loraB[32 * b:32 * b + R2, :],
                                 c2_B[bass.ds(a, 1)].rearrange("a r n -> r (a n)")).then_inc(s_lb, 16)
                for m in range(W_CHUNKS):
                    s = wi(m)
                    if m < 2:
                        sp.wait_ge(s_cond, i * KB + KB)
                    elif m < 4:
                        sp.wait_ge(s_w2lo, i * KB + KB)
                        sp.wait_ge(s_w2hi, i * KB + KB)
                    else:
                        sp.wait_ge(s_wf, i * W_CHUNKS + m - 3)
                    n = 512 if m == W_CHUNKS - 1 and I_TILES % 2 else 1024
                    src = gu_q[m] if m < I_TILES else dn_q[m - I_TILES, :, 0:n]
                    sp.dma_start(stage[:, s, 0:n].bitcast(I32), src).then_inc(s_wi[s], 16)
                for k in range(KB):
                    sp.wait_ge(s_y, i * KB + k + 1)
                    sp.dma_start(out[bass.ds(i, 1), :, k].rearrange("a p n -> p (a n)"),
                                 xres[:, k, :]).then_inc(s_out, 16)
                sp.wait_ge(s_out, i * (16 * KB) + 16 * KB)
                sp.sem_inc(s_gate_sp, 1)

        @block.scalar
        def _(act):
            act.dma_start(raw[:, 0:3584], proj_w).then_inc(s_raw[0], 16)
            for dst, src in ((rope[:, :, :], rope_tab), (maskq[:, :], causal), (eyef[:, :], eye),
                             (keyrow[:, :], key_rows), (headcol[:, :], head_cols), (scale[:, :], scales),
                             (bias2[:, :], c2_b)):
                act.dma_start(dst, src).then_inc(s_const, 16)
            act.dma_start(raw[:, 3584:5632], wo_w).then_inc(s_raw[1], 16)
            act.dma_start(raw[:, 5632:6144], gA).then_inc(s_raw[2], 16)
            act.dma_start(raw[:, 6144:6656], uA).then_inc(s_raw[2], 16)
            act.dma_start(raw[:, 6656:8064], gB).then_inc(s_raw[3], 16)
            act.dma_start(raw[:, 8064:9472], uB).then_inc(s_raw[3], 16)
            act.dma_start(raw[:, 9472:9824], dA).then_inc(s_raw[4], 16)
            act.dma_start(raw[:, 9824:10336], dB).then_inc(s_raw[4], 16)
            act.wait_ge(s_raw[0], 16)
            nc.scalar.activation(projw[:, 0, :, :], r_proj, ACT.Copy).then_inc(s_hi0, 1)
            act.wait_ge(s_raw[1], 16)
            nc.scalar.activation(wow[:, 0, :, :], r_wo, ACT.Copy).then_inc(s_hi0, 1)
            act.wait_ge(s_raw[2], 32)
            nc.scalar.activation(guA[:, 0, :, :, :].rearrange("p w k n -> p (w k n)"), raw[:, 5632:6656], ACT.Copy).then_inc(s_hi0, 1)
            act.wait_ge(s_raw[3], 32)
            nc.scalar.activation(guB[:, :, :], r_guB, ACT.Copy).then_inc(s_hi0, 1)
            act.wait_ge(s_raw[4], 32)
            for c in (0, 2):
                nc.scalar.activation(dnA[:, :, c, :], r_dnA, ACT.Copy).then_inc(s_hi0, 1)
            nc.scalar.activation(dnB[:, 0, :], r_dnB, ACT.Copy).then_inc(s_hi0, 1)
            with act.Fori(0, HALVES) as i:
                for k in range(KB):
                    act.wait_ge(s_cond, i * KB + k + 1)
                    nc.scalar.activation(xc[:, 0, k, :], bank[k][:, :], ACT.Copy).then_inc(s_xchi, 1)
                act.wait_ge(s_const, 16 * 7)
                for t in range(2):
                    act.wait_ge(s_rope, i * 6 + t + 1)
                    if t == 0:
                        act.wait_ge(s_split, 8)
                    for g in range(4):
                        nc.scalar.activation(km[:, 0, 4 * t + g, :], slots[:, 2 + t, :], ACT.Copy,
                                             scale=keyrow[:, g:g + 1]).then_inc(s_kmhi, 1)
                for j in range(GROUPS):
                    act.wait_ge(s_rope, i * 6 + j + 3)
                    nc.scalar.activation(qq[0:64, 0, j, :], slots[0:64, 4 + j, :], ACT.Copy).then_inc(s_qhi, 1)
                    nc.scalar.activation(qq[64:128, 1, j, :], slots[64:128, 4 + j, :], ACT.Copy).then_inc(s_qhi, 1)
                act.wait_ge(s_proj, i * PROJ + PROJ)
                nc.scalar.activation(nrm[:, 0, :], bank[2][:, :], ACT.Copy).then_inc(s_vT, 1)

                def attention_hi(b):
                    act.wait_ge(s_on, i * NB + b + 1)
                    nc.scalar.activation(att[:, 0, :, S * b:S * b + S],
                                         nrm[:, b % 2, :].rearrange("p (j n) -> p j n", j=GROUPS),
                                         ACT.Copy).then_inc(s_ahi, 1)

                for b in range(NB):
                    for n in range(NKV):
                        act.wait_ge(s_ST, i * 32 + 8 * b + n + 1)
                        if b:
                            act.wait_ge(s_pused, i * 8 + 2 * b - (1 if n < 4 else 0))
                        nc.scalar.activation(slots[:, n, :], bank[(6, 7, 3)[(8 * b + n) % 3]][:, :], ACT.Exp,
                                             scale=QK_SCALE).then_inc(s_exp, 1)
                    if b:
                        attention_hi(b - 1)
                attention_hi(NB - 1)
                act.wait_ge(s_ST, i * 32 + 32)
                act.wait_ge(s_w2raw, i * 16 + 16)
                for k in range(KB):
                    nc.scalar.activation(w2[:, 0, k, :], stage[:, k // 2, 512 * (k % 2):512 * (k % 2) + 512],
                                         ACT.Copy).then_inc(s_w2hi, 1)
                for k in range(KB):
                    act.wait_ge(s_x1, i * KB + k + 1)
                    nc.scalar.activation(x1[:, 0, k, :], xres[:, k, :], ACT.Copy).then_inc(s_x1hi, 1)
                for k in range(KB):
                    act.wait_ge(s_c2, i * KB + k + 1)
                    nc.scalar.activation(xb[:, 0, k, :], bank[k][:, :], ACT.Identity,
                                         bias=bias2[:, k:k + 1]).then_inc(s_xbhi, 1)

                def tanh(n):
                    act.wait_ge(s_g, i * I_TILES + n + 1)
                    nc.scalar.activation(slots[:, 4 + n % 2, :], slots[:, n % 2, :], ACT.Tanh,
                                         scale=0.5).then_inc(s_th, 1)

                def hidden_hi(n):
                    act.wait_ge(s_h, i * I_TILES + n + 1)
                    nc.scalar.activation(hid(n, 0), slots[:, 2 + n % 2, :], ACT.Copy).then_inc(s_hhi, 1)

                for n in range(I_TILES):
                    gate, up = bank[4 * (n % 2)], bank[4 * (n % 2) + 1]
                    act.wait_ge(s_gu, i * I_TILES + n + 1)
                    if n >= 2:
                        act.wait_ge(s_h1, i * I_TILES + n - 1)
                    nc.scalar.activation(slots[:, n % 2, :], gate[:, :], ACT.Copy,
                                         scale=scale[:, n:n + 1]).then_inc(s_tgu, 1)
                    if n >= 2:
                        hidden_hi(n - 2)
                        act.wait_ge(s_hlo, i * I_TILES + n - 1)
                        act.wait_ge(s_hhi, i * I_TILES + n - 1)
                    nc.scalar.activation(slots[:, 2 + n % 2, :], up[:, :], ACT.Copy,
                                         scale=scale[:, I_TILES + n:I_TILES + n + 1]).then_inc(s_tgu, 1)
                    if n >= 1:
                        tanh(n - 1)
                tanh(I_TILES - 1)
                hidden_hi(I_TILES - 2)
                hidden_hi(I_TILES - 1)

        @block.gpsimd
        def _(pool):
            nc.gpsimd.memset(vpad[:, :, :, :], 0.0).then_inc(s_zeros, 1)
            nc.gpsimd.memset(ones2[:, :, :], 0.0).then_inc(s_zeros, 1)
            nc.gpsimd.memset(lorah[:, :], 0.0).then_inc(s_zeros, 1)
            nc.gpsimd.memset(loraB[:, :], 0.0).then_inc(s_zeros, 1)
            pool.wait_ge(s_zeros, 4)
            nc.gpsimd.memset(ones2[:, 0, 0:16], 1.0).then_inc(s_zeros, 1)
            nc.gpsimd.memset(ones2[:, 1, 16:32], 1.0).then_inc(s_zeros, 1)
            pool.wait_ge(s_const, 16 * 7)
            with pool.Fori(0, HALVES) as i:
                for t in range(6):
                    pool.wait_ge(s_sw, i * 6 + t + 1)
                    sw = slots[:, t % 2, :].rearrange("p (b n) -> p b n", b=NB)
                    sin = rope[:, 1:2, :].broadcast_to([P, NB, S])
                    nc.gpsimd.tensor_tensor(sw, sw, sin, ALU.mult).then_inc(s_sin, 1)
                    pool.wait_ge(s_sin, i * 6 + t + 1)
                    pool.wait_ge(s_cos, i * 6 + t + 1)
                    nc.gpsimd.tensor_tensor(slots[:, 2 + t, :], slots[:, 2 + t, :], slots[:, t % 2, :],
                                            ALU.add).then_inc(s_rope, 1)

                def attention_lo(b):
                    pool.wait_ge(s_ahi, i * NB + b + 1)
                    nc.gpsimd.tensor_tensor(att[:, 1, :, S * b:S * b + S],
                                            nrm[:, b % 2, :].rearrange("p (j n) -> p j n", j=GROUPS),
                                            f(att[:, 0, :, S * b:S * b + S]), ALU.subtract).then_inc(s_alo, 1)

                for b in range(NB):
                    for n in range(NKV):
                        pool.wait_ge(s_exp, i * 32 + 8 * b + n + 1)
                        pool.sem_inc(s_gate_pool, 1)
                        p = slots[:, n, :].rearrange("p (j q) -> p j q", j=GROUPS)
                        nc.gpsimd.affine_select(out=p, in_=p, compare_op=ALU.is_ge, fill=0.0, base=0,
                                                pattern=[[0, GROUPS], [1, S]],
                                                channel_multiplier=-1).then_inc(s_p, 1)
                    if b:
                        attention_lo(b - 1)
                attention_lo(NB - 1)
                for k in range(KB):
                    pool.wait_ge(s_w2hi, i * KB + k + 1)
                    nc.gpsimd.tensor_tensor(w2[:, 1, k, :], stage[:, k // 2, 512 * (k % 2):512 * (k % 2) + 512],
                                            f(w2[:, 0, k, :]), ALU.subtract).then_inc(s_w2lo, 1)

                def convert(m):
                    s = wi(m)
                    n = 512 if m == W_CHUNKS - 1 and I_TILES % 2 else 1024
                    pool.wait_ge(s_wi[s], i * (16 * wi_uses[s]) + 16 * (m // 4 + 1))
                    if 2 <= m < I_TILES + 2:
                        pool.wait_ge(s_gu, i * I_TILES + m - 1)
                    elif m >= I_TILES + 2:
                        pool.wait_ge(s_dn, i * D_CHUNKS + m - I_TILES - 1)
                    pool.sem_inc(s_gate_pool, 1)
                    nc.gpsimd.tensor_scalar(wf[:, m % 2, 0:n], stage[:, s, 0:n].bitcast(I32), -Q_ZERO, None,
                                            ALU.add).then_inc(s_wf, 1)

                for k in range(KB):
                    pool.wait_ge(s_x1hi, i * KB + k + 1)
                    nc.gpsimd.tensor_tensor(x1[:, 1, k, :], xres[:, k, :], f(x1[:, 0, k, :]),
                                            ALU.subtract).then_inc(s_x1lo, 1)
                convert(0)
                convert(1)

                def hidden_lo(n):
                    pool.wait_ge(s_hhi, i * I_TILES + n + 1)
                    nc.gpsimd.tensor_tensor(hid(n, 1), slots[:, 2 + n % 2, :], f(hid(n, 0)),
                                            ALU.subtract).then_inc(s_hlo, 1)

                for n in range(I_TILES):
                    convert(n + 2)
                    if n >= 2:
                        hidden_lo(n - 2)
                hidden_lo(I_TILES - 2)
                hidden_lo(I_TILES - 1)
                for m in range(I_TILES + 2, W_CHUNKS):
                    convert(m)

        @block.vector
        def _(dve):
            dve.wait_ge(s_hi0, 1)
            nc.vector.tensor_tensor(projw[:, 1, :, :], r_proj, f(projw[:, 0, :, :]), ALU.subtract).then_inc(s_split, 1)
            dve.wait_ge(s_hi0, 2)
            nc.vector.tensor_tensor(wow[:, 1, :, :], r_wo, f(wow[:, 0, :, :]), ALU.subtract).then_inc(s_split, 1)
            dve.wait_ge(s_hi0, 3)
            nc.vector.tensor_tensor(guA[:, 1, :, :, :].rearrange("p w k n -> p (w k n)"), raw[:, 5632:6656],
                                    f(guA[:, 0, :, :, :].rearrange("p w k n -> p (w k n)")), ALU.subtract).then_inc(s_split, 1)
            dve.wait_ge(s_hi0, 4)
            for r0 in (32, 96):
                nc.vector.tensor_tensor(guB[r0:r0 + 32, :, :], r_guB[r0:r0 + 32], f(guB[r0:r0 + 32, :, :]),
                                        ALU.subtract).then_inc(s_split, 1)
            dve.wait_ge(s_hi0, 7)
            for c in (1, 3):
                nc.vector.tensor_tensor(dnA[:, :, c, :], r_dnA, f(dnA[:, :, 0, :]), ALU.subtract).then_inc(s_split, 1)
            nc.vector.tensor_tensor(dnB[:, 1, :], r_dnB, f(dnB[:, 0, :]), ALU.subtract).then_inc(s_split, 1)
            dve.wait_ge(s_const, 16 * 7)
            nc.vector.tensor_scalar(scale[:, :], scale[:, :], Q_STEP, None, ALU.mult).then_inc(s_init, 1)
            nc.vector.tensor_copy(eyeb[:, :], eyef[:, :]).then_inc(s_init, 1)
            nc.vector.tensor_reduce(headrow[:, :], eyef[0:NH, 0:NH].rearrange("h (g j) -> h g j", j=GROUPS),
                                    AX_X, ALU.max).then_inc(s_headrow, 1)
            dve.wait_ge(s_headrow, 1)
            nc.vector.tensor_copy(headsel[:, :, :], headrow[:, :].rearrange("h (g o) -> h g o", o=1)
                                  .broadcast_to([NH, NKV, P])).then_inc(s_init, 1)
            with dve.Fori(0, HALVES) as i:
                for k in range(KB):
                    dve.wait_ge(s_xchi, i * KB + k + 1)
                    nc.vector.tensor_tensor(xc[:, 1, k, :], bank[k][:, :], f(xc[:, 0, k, :]),
                                            ALU.subtract).then_inc(s_xclo, 1)

                def rotate(t):
                    ps = bank[(4, 5, 6, 7, 0, 1)[t]]
                    dve.wait_ge(s_proj, i * PROJ + t + 1)
                    if t >= 2:
                        dve.wait_ge(s_rope, i * 6 + t - 1)
                    dve.sem_inc(s_gate_dve, 1)
                    nc.vector.stream_shuffle(slots[:, t % 2, :], ps[:, :],
                                             [16 * (p // 16) + (p + 8) % 16 for p in range(32)]).then_inc(s_sw, 1)
                    cos = rope[:, 0:1, :].broadcast_to([P, NB, S])
                    nc.vector.tensor_tensor(slots[:, 2 + t, :].rearrange("p (b n) -> p b n", b=NB),
                                            ps[:, :].rearrange("p (b n) -> p b n", b=NB), cos,
                                            ALU.mult).then_inc(s_cos, 1)

                def k_lo(t):
                    for g in range(4):
                        dve.wait_ge(s_kmhi, i * 8 + 4 * t + g + 1)
                        nc.vector.scalar_tensor_tensor(out=km[:, 1, 4 * t + g, :], in0=slots[:, 2 + t, :],
                                                       scalar=keyrow[:, g:g + 1], in1=f(km[:, 0, 4 * t + g, :]),
                                                       op0=ALU.mult, op1=ALU.subtract).then_inc(s_kmlo, 1)

                def q_lo(j):
                    dve.wait_ge(s_qhi, i * 8 + 2 * j + 2)
                    nc.vector.tensor_tensor(qq[64:128, 0, j, :], slots[0:64, 4 + j, :], f(qq[0:64, 0, j, :]),
                                            ALU.subtract).then_inc(s_qlo, 1)
                    nc.vector.tensor_tensor(qq[0:64, 1, j, :], slots[64:128, 4 + j, :], f(qq[64:128, 1, j, :]),
                                            ALU.subtract).then_inc(s_qlo, 1)

                rotate(0)
                rotate(1)
                rotate(2)
                rotate(3)
                k_lo(0)
                rotate(4)
                k_lo(1)
                rotate(5)
                for j in range(GROUPS):
                    q_lo(j)
                dve.wait_ge(s_vtr, i + 1)
                vt = bank[3][:, :].rearrange("p (b m c d) -> p b m c d", b=NB, m=PAIRS, c=2)
                vp = vpad[:, :, :, :].rearrange("p b (m c) n -> p b m c n", c=2)
                for c in range(2):
                    nc.vector.tensor_copy(vp[:, :, :, c, 16 * c:16 * c + 16], vt[:, :, :, c, :]).then_inc(s_v, 1)

                def normalise(b):
                    dve.wait_ge(s_pused, i * 8 + 2 * b + 2)
                    if b >= 2:
                        dve.wait_ge(s_alo, i * NB + b - 1)
                    nc.vector.reciprocal(nrm[:, b % 2, :], bank[1][:, :]).then_inc(s_rec, 1)
                    dve.wait_ge(s_rec, i * NB + b + 1)
                    nc.vector.tensor_tensor(nrm[:, b % 2, :], bank[0][:, :], nrm[:, b % 2, :],
                                            ALU.mult).then_inc(s_on, 1)

                for b in range(NB):
                    for n in range(8):
                        t, j = n // 4, n % 4
                        dve.wait_ge(s_S, i * 32 + 8 * b + n + 1)
                        nc.vector.tensor_reduce(mx[:, b % 2, 4 * t:4 * t + 4, j],
                                                bank[4 + n % 2][:, :].rearrange("p (g k) -> p g k", g=4),
                                                AX_X, ALU.max).then_inc(s_max, 1)
                    dve.wait_ge(s_mT, i * NB + b + 1)
                    if b:
                        dve.wait_ge(s_ST, i * 32 + 8 * b)
                    mt = bank[2][0:NH, 0:S].rearrange("h (o q) -> h o q", o=1).broadcast_to([NH, GROUPS, S])
                    sel = headcol[:, :].rearrange("h (j o) -> h j o", o=1).broadcast_to([NH, GROUPS, S])
                    nc.vector.tensor_tensor(shift[:, :, :], mt, sel, ALU.mult).then_inc(s_shift, 1)
                    if b:
                        normalise(b - 1)
                normalise(NB - 1)
                for k in range(KB):
                    dve.wait_ge(s_wo, i * KB + k + 1)
                    nc.vector.tensor_tensor(xres[:, k, :], bank[4 + k][:, :], xres[:, k, :],
                                            ALU.add).then_inc(s_x1, 1)
                dve.wait_ge(s_zeros, 4)
                for b in range(NB):
                    dve.wait_ge(s_lh, i * NB + b + 1)
                    nc.vector.tensor_scalar(lorah[32 * b:32 * b + R2, S * b:S * b + S], bank[4][32 * b:32 * b + R2, 0:S],
                                            LORA_SCALE, None, ALU.mult).then_inc(s_lhs, 1)
                for k in range(KB):
                    dve.wait_ge(s_xbhi, i * KB + k + 1)
                    nc.vector.scalar_tensor_tensor(out=xb[:, 1, k, :], in0=bank[k][:, :], scalar=bias2[:, k:k + 1],
                                                   in1=f(xb[:, 0, k, :]), op0=ALU.add,
                                                   op1=ALU.subtract).then_inc(s_xblo, 1)

                def low_rank(k, w, ps):
                    dve.wait_ge(s_zp, i * 3 + k + 1)
                    nc.vector.tensor_copy(z[:, w, :], ps[:, :]).then_inc(s_zhi, 1)
                    dve.wait_ge(s_zhi, i * 3 + k + 1)
                    nc.vector.tensor_tensor(z[64:128, w, :], ps[64:128, :], f(z[64:128, w, :]),
                                            ALU.subtract).then_inc(s_z, 1)

                low_rank(0, 0, bank[5])
                low_rank(1, 1, bank[6])

                def hidden(n):
                    dve.wait_ge(s_th, i * I_TILES + n + 1)
                    nc.vector.scalar_tensor_tensor(out=slots[:, 4 + n % 2, :], in0=slots[:, 4 + n % 2, :], scalar=1.0,
                                                   in1=slots[:, n % 2, :], op0=ALU.add,
                                                   op1=ALU.mult).then_inc(s_h1, 1)
                    dve.wait_ge(s_h1, i * I_TILES + n + 1)
                    nc.vector.scalar_tensor_tensor(out=slots[:, 2 + n % 2, :], in0=slots[:, 4 + n % 2, :], scalar=0.5,
                                                   in1=slots[:, 2 + n % 2, :], op0=ALU.mult,
                                                   op1=ALU.mult).then_inc(s_h, 1)

                for n in range(I_TILES):
                    gl, ul = bank[4 * (n % 2) + 2], bank[4 * (n % 2) + 3]
                    dve.wait_ge(s_tgu, i * (2 * I_TILES) + 2 * n + 1)
                    nc.vector.scalar_tensor_tensor(out=slots[:, n % 2, :], in0=gl[:, :], scalar=LR_SCALE,
                                                   in1=slots[:, n % 2, :], op0=ALU.mult,
                                                   op1=ALU.add).then_inc(s_g, 1)
                    dve.wait_ge(s_tgu, i * (2 * I_TILES) + 2 * n + 2)
                    nc.vector.scalar_tensor_tensor(out=slots[:, 2 + n % 2, :], in0=ul[:, :], scalar=LR_SCALE,
                                                   in1=slots[:, 2 + n % 2, :], op0=ALU.mult,
                                                   op1=ALU.add).then_inc(s_u, 1)
                    if n:
                        dve.wait_ge(s_u, i * I_TILES + n)
                        hidden(n - 1)
                dve.wait_ge(s_u, i * I_TILES + I_TILES)
                hidden(I_TILES - 1)
                low_rank(2, 0, bank[0])
                for k in range(KB):
                    if k == 0:
                        dve.wait_ge(s_dn, i * D_CHUNKS + D_CHUNKS)
                    nc.vector.scalar_tensor_tensor(out=xres[:, k, :], in0=bank[4 + k][:, :],
                                                   scalar=scale[:, 2 * I_TILES + k:2 * I_TILES + k + 1],
                                                   in1=xres[:, k, :], op0=ALU.mult, op1=ALU.add).then_inc(s_r1, 1)
                for k in range(KB):
                    dve.wait_ge(s_r1, i * KB + k + 1)
                    dve.wait_ge(s_dl, i * KB + k + 1)
                    nc.vector.scalar_tensor_tensor(out=xres[:, k, :], in0=bank[k][:, :], scalar=LR_SCALE,
                                                   in1=xres[:, k, :], op0=ALU.mult, op1=ALU.add).then_inc(s_y, 1)

        @block.tensor
        def _(pe):
            mm = nc.tensor.matmul

            def split3(ps, whi, wlo, xhi, xlo, start, stop):
                mm(ps, whi, xhi, start=start, stop=False)
                mm(ps, whi, xlo, start=False, stop=False)
                return mm(ps, wlo, xhi, start=False, stop=stop)

            pe.wait_ge(s_zeros, 6)
            pe.wait_ge(s_init, 3)
            with pe.Fori(0, HALVES) as i:
                pe.wait_ge(s_x, i * 16 + 16)
                for b in range(NB):
                    pe.wait_ge(s_wc[b % 2], i * 32 + 16 * (b // 2 + 1))
                    w = stage[:, 2 * (b % 2):2 * (b % 2) + 2, :].rearrange("p a n -> p (a n)").rearrange(
                        "p (k n) -> p k n", k=KB)
                    for o in range(KB):
                        for k in range(KB):
                            last = mm(bank[o][:, S * b:S * b + S], w[:, k, P * o:P * o + P],
                                      xres[:, k, S * b:S * b + S], start=(k == 0), stop=(k == KB - 1))
                        if b == NB - 1:
                            last.then_inc(s_cond, 1)
                    if b < NB - 1:
                        last.then_inc(s_condb, 1)

                pe.wait_ge(s_split, 8)

                def project(t, ps, k):
                    return split3(ps[:, :], projw[:, 0, k, P * t:P * t + P], projw[:, 1, k, P * t:P * t + P],
                                  xc[:, 0, k, :], xc[:, 1, k, :], k == 0, k == KB - 1)

                for k in range(KB):
                    pe.wait_ge(s_xclo, i * KB + k + 1)
                    for t in range(4):
                        last = project(t, bank[4 + t], k)
                        if k == KB - 1:
                            last.then_inc(s_proj, 1)
                for t in range(4, PROJ):
                    for k in range(KB):
                        last = project(t, bank[t - 4], k)
                    last.then_inc(s_proj, 1)

                def scores(b, n):
                    t, j = n // 4, n % 4
                    ps = bank[4 + n % 2]
                    if b == 0 and n == 0:
                        pe.wait_ge(s_kmlo, i * 8 + 8)
                        pe.wait_ge(s_kmhi, i * 8 + 8)
                    if b == 0:
                        pe.wait_ge(s_qlo, i * 8 + (2 * j + 2 if t == 0 else 8))
                    if 8 * b + n >= 2:
                        pe.wait_ge(s_max, i * 32 + 8 * b + n - 1)
                    mm(ps[:, :], eyeb[:, :], maskq[:, :], start=True, stop=False)
                    mm(ps[:, :], qq[:, t, j, S * b:S * b + S], km[:, 0, 4 * t:4 * t + 4, S * b:S * b + S],
                       start=False, stop=True).then_inc(s_S, 1)

                def turn_max(b):
                    pe.wait_ge(s_max, i * 32 + 8 * b + 8)
                    if b:
                        pe.wait_ge(s_shift, i * NB + b)
                    nc.tensor.transpose(bank[2][0:NH, 0:S], mx[:, b % 2, :, :].rearrange("p g j -> p (g j)"),
                                        eyef[:, :]).then_inc(s_mT, 1)

                def scores_turned(b, n):
                    g = ST_ORDER[n]
                    ps = bank[(6, 7, 3)[(8 * b + n) % 3]]
                    if b == 0 and n == 0:
                        pe.wait_ge(s_v, i * 2 + 2)
                    if n == 0:
                        pe.wait_ge(s_shift, i * NB + b + 1)
                    if 8 * b + n >= 3:
                        pe.wait_ge(s_exp, i * 32 + 8 * b + n - 2)
                    q = qq[:, g // 4, :, S * b:S * b + S]
                    mm(ps[:, :], km[:, 0, g, S * b:S * b + S], q, start=True, stop=False)
                    mm(ps[:, :], km[:, 1, g, S * b:S * b + S], q, start=False, stop=False)
                    mm(ps[:, :], headsel[:, g, :], shift[:, :, :].rearrange("h j q -> h (j q)"),
                       start=False, stop=True).then_inc(s_ST, 1)

                def values(b, c):
                    if c == 0 and b:
                        pe.wait_ge(s_on, i * NB + b)
                    pe.wait_ge(s_p, i * 32 + 8 * b + 4 * c + 4)
                    for w, ps in ((None, bank[0]), (ones2, bank[1])):
                        for m in range(PAIRS):
                            lhs = ones2[:, c, :] if w is not None else vpad[:, b, 2 * m + c, :]
                            last = mm(ps[32 * m:32 * m + 32, :], lhs, slots[:, 4 * c + m, :],
                                      start=(c == 0), stop=(c == 1), tile_position=(0, 32 * m))
                    last.then_inc(s_pused, 1)
                    return last

                pe.wait_ge(s_vT, i + 1)
                for b in range(NB):
                    last = nc.tensor.transpose(bank[3][:, S * b:S * b + S], nrm[:, 0, S * b:S * b + S], eyef[:, :])
                last.then_inc(s_vtr, 1)
                for n in range(8):
                    scores(0, n)
                for b in range(NB):
                    turn_max(b)
                    if b + 1 < NB:
                        for n in range(8):
                            scores(b + 1, n)
                    for n in range(8):
                        scores_turned(b, n)
                        if n == 6:
                            values(b, 0)
                    values(b, 1)

                pe.wait_ge(s_alo, i * NB + NB)
                for o in range(KB):
                    for j in range(KB):
                        last = split3(bank[4 + o][:, :], wow[:, 0, j, P * o:P * o + P], wow[:, 1, j, P * o:P * o + P],
                                      att[:, 0, j, :], att[:, 1, j, :], j == 0, j == KB - 1)
                    last.then_inc(s_wo, 1)
                pe.wait_ge(s_w2lo, i * KB + KB)
                for k in range(KB):
                    pe.wait_ge(s_x1lo, i * KB + k + 1)
                    for o in range(KB):
                        split3(bank[o][:, :], w2[:, 0, k, P * o:P * o + P], w2[:, 1, k, P * o:P * o + P],
                               x1[:, 0, k, :], x1[:, 1, k, :], k == 0, False)
                pe.wait_ge(s_la, i * (16 * NB) + 16 * NB)
                pe.wait_ge(s_lb, i * (16 * NB) + 16 * NB)
                for b in range(NB):
                    for k in range(KB):
                        last = mm(bank[4][32 * b:32 * b + R2, 0:S], loraA[:, b, k, :], xres[:, k, S * b:S * b + S],
                                  start=(k == 0), stop=(k == KB - 1), tile_position=(0, 32 * b))
                    last.then_inc(s_lh, 1)
                pe.wait_ge(s_lhs, i * NB + NB)
                for o in range(KB):
                    mm(bank[o][:, :], loraB[:, P * o:P * o + P], lorah[:, :], start=False,
                       stop=True).then_inc(s_c2, 1)
                for k in range(KB):
                    pe.wait_ge(s_xblo, i * KB + k + 1)
                    for w in range(2):
                        last = split3(bank[5 + w][:, :], guA[:, 0, w, k, :], guA[:, 1, w, k, :],
                                      xb[:, 0, k, :], xb[:, 1, k, :], k == 0, k == KB - 1)
                        if k == KB - 1:
                            last.then_inc(s_zp, 1)
                for n in range(I_TILES):
                    ps = [bank[4 * (n % 2) + c] for c in range(4)]
                    if n >= 2:
                        pe.wait_ge(s_u, i * I_TILES + n - 1)
                    if n == 1:
                        pe.wait_ge(s_z, i * 3 + 2)
                    pe.wait_ge(s_wf, i * W_CHUNKS + n + 1)
                    wt = wf[:, n % 2, :].rearrange("p (w k o) -> p w k o", w=2, k=KB)
                    for w in range(2):
                        for k in range(KB):
                            mm(ps[w][:, :], wt[:, w, k, :], xb[:, 0, k, :], start=(k == 0), stop=False)
                            mm(ps[w][:, :], wt[:, w, k, :], xb[:, 1, k, :], start=False, stop=(k == KB - 1))
                    if n == 0:
                        pe.wait_ge(s_z, i * 3 + 2)
                    for w in range(2):
                        last = mm(ps[2 + w][:, :], guB[:, w, P * n:P * n + P], z[:, w, :], start=True, stop=True)
                    last.then_inc(s_gu, 1)
                pe.wait_ge(s_u, i * I_TILES + I_TILES - 1)
                for c in range(D_CHUNKS):
                    m = I_TILES + c
                    pe.wait_ge(s_wf, i * W_CHUNKS + m + 1)
                    for n in range(2 * c, min(2 * c + 2, I_TILES)):
                        pe.wait_ge(s_hlo, i * I_TILES + n + 1)
                        for o in range(KB):
                            wt = wf[:, m % 2, 512 * (n % 2) + P * o:512 * (n % 2) + P * o + P]
                            mm(bank[4 + o][:, :], wt, hid(n, 0), start=(n == 0), stop=False)
                            last = mm(bank[4 + o][:, :], wt, hid(n, 1), start=False, stop=(n == I_TILES - 1))
                    last.then_inc(s_dn, 1)
                for n in range(I_TILES):
                    wt = dnA[:, n, :, :].rearrange("p c r -> p (c r)")
                    mm(bank[0][:, :], wt, hid(n, 0), start=(n == 0), stop=False)
                    last = mm(bank[0][:, :], wt, hid(n, 1), start=False, stop=(n == I_TILES - 1))
                last.then_inc(s_zp, 1)
                pe.wait_ge(s_z, i * 3 + 3)
                for o in range(KB):
                    mm(bank[o][:, :], dnB[:, 0, P * o:P * o + P], z[:, 0, :], start=True, stop=False)
                    mm(bank[o][:, :], dnB[:, 1, P * o:P * o + P], z[:, 0, :], start=False,
                       stop=True).then_inc(s_dl, 1)
                pe.wait_ge(s_y, i * KB + KB)


def kernel(**inputs):
    import numpy as np
    import ml_dtypes
    import concourse.bacc as bacc
    from concourse.bass_utils import run_bass_kernel_spmd

    a = {k: np.asarray(v) for k, v in inputs.items()}

    def blocks(w):
        return w.reshape(-1, P, w.shape[1]).transpose(1, 0, 2).reshape(P, -1)

    def pad(w, axis):
        n = IP - w.shape[axis]
        return np.pad(w, [(0, n if d == axis else 0) for d in range(w.ndim)])

    arrays = {}
    arrays["xT"] = a["x"].reshape(HALVES, T, KB, P).transpose(0, 3, 2, 1)
    arrays["ids"] = np.concatenate([a["itok_B_3_7"], a["itok_B_0_23"]]).reshape(1, 2 * B)
    arrays["cond_w"] = a["L0_cond_weight"].transpose(0, 2, 1).reshape(ADAPTERS, KB, P, H).transpose(
        0, 2, 1, 3).reshape(ADAPTERS, P, KB * H)
    wq = a["L0_attn_wq"].reshape(NKV, GROUPS, HD, H)
    wk = a["L0_attn_wk"].reshape(NKV, HD, H)
    rows = [np.tile(wk[4 * t:4 * t + 4].reshape(64, H), (2, 1)) for t in range(2)]
    rows += [wq[:, j].reshape(P, H) for j in range(GROUPS)] + [a["L0_attn_wv"]]
    arrays["proj_w"] = blocks(np.concatenate(rows).T)
    wo = a["L0_attn_wo"].T.reshape(NKV, GROUPS, HD, H).transpose(1, 0, 2, 3).reshape(H, H)
    arrays["wo_w"] = blocks(wo)
    arrays["c2_w"] = blocks(a["L0_cond2_W"].T)
    arrays["c2_b"] = a["L0_cond2_b"].reshape(KB, P).T
    arrays["c2_A"] = a["L0_cond2_lora_As"].reshape(SLOTS, KB, P, R2).transpose(0, 2, 1, 3).reshape(SLOTS, P, KB * R2)
    arrays["c2_B"] = a["L0_cond2_lora_Bs"]
    gu = np.stack([pad(a[f"L0_ffn_{n}_q"], 0) for n in ("gate", "up")])
    arrays["gu_q"] = gu.reshape(2, I_TILES, P, KB, P).transpose(1, 4, 0, 3, 2).reshape(I_TILES, P, 2 * KB * P)
    dn = pad(a["L0_ffn_down_q"].T, 0)
    dn = np.pad(dn, [(0, (2 * D_CHUNKS - I_TILES) * P), (0, 0)])
    arrays["dn_q"] = dn.reshape(D_CHUNKS, 2, P, H).transpose(0, 2, 1, 3).reshape(D_CHUNKS, P, 2 * H)
    arrays["scales"] = np.concatenate(
        [pad(a[f"L0_ffn_{n}_scale"], 0).reshape(I_TILES, P).T for n in ("gate", "up")]
        + [a["L0_ffn_down_scale"].reshape(KB, P).T], axis=1)
    arrays["gA"] = blocks(np.tile(a["L0_ffn_gate_A"], (1, 4)))
    arrays["uA"] = blocks(np.tile(a["L0_ffn_up_A"], (1, 4)))
    arrays["gB"] = np.tile(pad(a["L0_ffn_gate_B"], 1), (4, 1))
    arrays["uB"] = np.tile(pad(a["L0_ffn_up_B"], 1), (4, 1))
    arrays["dA"] = blocks(pad(a["L0_ffn_down_A"], 0))
    arrays["dB"] = np.tile(a["L0_ffn_down_B"], (4, 1))
    freq = (1.0 / np.float32(10000.0) ** (np.arange(0, HD, 2, dtype=np.float32) / np.float32(HD))).astype(np.float32)
    angle = np.arange(S, dtype=np.float32)[None, :] * np.concatenate([freq, freq])[:, None]
    sign = np.where(np.arange(HD) < HD // 2, -1.0, 1.0).astype(np.float32)[:, None]
    arrays["rope_tab"] = np.tile(np.stack([np.cos(angle), np.sin(angle) * sign], 1), (P // HD, 1, 1)).astype(np.float32)
    q, k = np.arange(S)[:, None], np.arange(S)[None, :]
    arrays["causal"] = np.tile(np.where(k <= q, 0.0, MASKED), (1, NB)).astype(ml_dtypes.bfloat16)
    arrays["eye"] = np.eye(P, dtype=np.float32)
    arrays["key_rows"] = (np.arange(P)[:, None] % 64 // HD == np.arange(4)).astype(np.float32)
    arrays["head_cols"] = -(np.arange(NH)[:, None] % GROUPS == np.arange(GROUPS)).astype(np.float32)

    nc = bacc.Bacc("TRN2", target_bir_lowering=False, num_devices=1)
    aps, ins = {}, {}
    for name, v in arrays.items():
        v = np.ascontiguousarray(v)
        ins[f"in_{name}_dram"] = v
        aps[name] = nc.dram_tensor(f"in_{name}_dram", v.shape, mybir.dt.from_np(v.dtype), kind="ExternalInput").ap()
    out = nc.dram_tensor("out_0_dram", (HALVES, P, KB, T), F32, kind="ExternalOutput").ap()
    adaln_attn_ffn(nc, out=out, **aps)
    r = run_bass_kernel_spmd(nc, [ins], core_ids=[0])
    got = r.results[0]["out_0_dram"]
    return np.ascontiguousarray(got.transpose(0, 3, 2, 1)).reshape(B, S, H)
```

```python
from contextlib import ExitStack

import concourse.bass as bass
from concourse import mybir

ALU = mybir.AluOpType
ACT = mybir.ActivationFunctionType
AX_X = mybir.AxisListType.X
F32 = mybir.dt.float32
F32R = mybir.dt.float32r
BF16 = mybir.dt.bfloat16
I32 = mybir.dt.int32

P = 128
H = 512
KB = H // P
B, S = 8, 128
HALVES = 2
NB = B // HALVES
T = NB * S
NH, NKV, HD = 32, 8, 16
GROUPS = NH // NKV
PAIRS = NKV // 2
QK_SCALE = HD ** -0.5
ADAPTERS, SLOTS, R2 = 8, 32, 16
R = 32
I_TILES = 11
IP = I_TILES * P
PROJ = 7
Q_ZERO, Q_STEP, LR_SCALE, LORA_SCALE = 7.5, 0.005, 0.02, 2.0
D_CHUNKS = (I_TILES + 1) // 2
W_CHUNKS = I_TILES + D_CHUNKS
U_CHUNKS = W_CHUNKS - I_TILES % 2
PROJ_BANK = (4, 5, 6, 7, 0, 1, 2)
ST_BANK = (6, 7, 3)
LEAD = 10
ON = NB - 1 + GROUPS
ST_ORDER = [0, 2, 4, 6, 1, 3, 5, 7]
MASKED = -1e30


def adaln_attn_ffn(nc, xT, ids, cond_w, proj_w, wo_w, c2_w, c2_b, c2_A, c2_B, gu_q, dn_q, scales,
                   gA, uA, gB, uB, dA, dB, rope_tab, causal, eye, key_rows, head_cols, out):
    with ExitStack() as ctx:
        def sb(name, shape, dt):
            return ctx.enter_context(nc.sbuf_tensor(name, shape, dt))

        def sem(name):
            return ctx.enter_context(nc.semaphore(name))

        bank = [ctx.enter_context(nc.psum_tensor(f"bank{k}", [P, T], F32)) for k in range(8)]

        projw = sb("projw", [P, 2, KB, PROJ * P], F32R)
        wow = sb("wow", [P, 2, KB, H], F32R)
        guA = sb("guA", [P, 2, 2, KB, P], F32R)
        guB = sb("guB", [P, 2, IP], F32R)
        dnA = sb("dnA", [P, I_TILES, 4, R], F32R)
        dnB = sb("dnB", [P, 2, H], F32R)
        headsel = sb("headsel", [NH, NKV, P], F32R)
        rope = sb("rope", [P, 2, S], F32)
        maskq = sb("maskq", [P, NB * S], BF16)
        eyef = sb("eyef", [P, P], F32)
        eyeb = sb("eyeb", [P, P], BF16)
        keyrow = sb("keyrow", [P, 4], F32)
        headcol = sb("headcol", [NH, GROUPS], F32)
        headrow = sb("headrow", [NH, NKV], F32)
        ones2 = sb("ones2", [P, 2, 32], F32)
        scale = sb("scale", [P, 2 * I_TILES + KB], F32)
        bias2 = sb("bias2", [P, KB], F32)
        ids_sb = sb("ids_sb", [1, 2 * B], I32)
        xres = sb("xres", [P, KB, T], F32)
        stage = sb("stage", [P, 4, 1024], F32)
        wf = sb("wf", [P, 2, 1024], F32R)
        vpad = sb("vpad", [P, NB, NKV, 32], F32)
        slots = sb("slots", [P, 8, T], F32)
        nrm = sb("nrm", [P, 2, T], F32)
        shift = sb("shift", [NH, GROUPS, S], F32R)
        mx = sb("mx", [P, 2, NKV, GROUPS], F32)
        loraA = sb("loraA", [P, NB, KB, R2], F32)
        loraB = sb("loraB", [P, H], F32)
        lorah = sb("lorah", [P, T], F32)
        xc = sb("xc", [P, 2, KB, T], F32R)
        with nc.sbuf_tensor("rawp", [P, KB, PROJ * P], F32) as raw_proj:
            pass
        arena = sb("arena", [P, 3 * 4096], F32R)

        att = xc
        qq = arena[:, 0:4096].rearrange("p (t j n) -> p t j n", t=2, j=GROUPS)
        x1 = arena[:, 0:4096].rearrange("p (a k n) -> p a k n", a=2, k=KB)
        km = arena[:, 4096:12288].rearrange("p (a g n) -> p a g n", a=2, g=NKV)
        xb = arena[:, 4096:8192].rearrange("p (a k n) -> p a k n", a=2, k=KB)
        w2 = arena[:, 8192:12288].rearrange("p (a k n) -> p a k n", a=2, k=KB)
        z = arena[:, 11264:12288].rearrange("p (w n) -> p w n", w=2)
        xcf = xc[:, :, :, :].rearrange("p a k n -> p (a k n)")
        stage_flat = stage[:, :, :].rearrange("p a n -> p (a n)")
        slots_flat = slots[:, :, :].rearrange("p a n -> p (a n)")
        adapter = [stage_flat[:, 0:2048], stage_flat[:, 2048:4096], slots_flat[:, 2048:4096], slots_flat[:, 0:2048]]
        raw_w2 = stage_flat[:, 0:2048].rearrange("p (k n) -> p k n", k=KB)
        raw_wo = stage_flat[:, 2048:4096].rearrange("p (k n) -> p k n", k=KB)
        raw_B = stage_flat[:, 2048:2048 + IP]
        raw_dB = stage_flat[:, 2048 + IP:2048 + IP + H]
        raw_dA = stage_flat[:, 2048 + IP:2048 + IP + I_TILES * R].rearrange("p (n r) -> p n r", r=R)
        raw_guA = stage_flat[:, 2048:3072].rearrange("p (w k n) -> p w k n", w=2, k=KB)
        U_SLOT = (2, 3, 6, 7)

        def hid(n, part):
            if n < 4:
                return xcf[:, 1024 * n + 512 * part:1024 * n + 512 * part + 512]
            at = (1024 * (n - 4) if n < 8 else 8192 + 1024 * (n - 8)) + 512 * part
            return arena[:, at:at + 512]

        def f(ap):
            return ap.bitcast(F32)

        def wi(m):
            return (m + 2) % 4

        wi_uses = [len([m for m in range(W_CHUNKS) if wi(m) == s]) for s in range(4)]

        def wait_convert(eng, i, m):
            s = wi(m)
            eng.wait_ge(s_wi[s], 16 * (i * wi_uses[s] + m // 4 + 1))
            if 2 <= m < I_TILES + 2:
                eng.wait_ge(s_gu, i * I_TILES + m - 1)
            elif m >= I_TILES + 2:
                eng.wait_ge(s_dn, i * D_CHUNKS + m - I_TILES - 1)

        s_wi = [sem(f"s_wi{n}") for n in range(4)]
        s_gu = sem("s_gu")
        s_dn = sem("s_dn")
        s_wc = [sem(f"s_wc{n}") for n in range(NB)]
        s_x = sem("s_x")
        s_ids = sem("s_ids")
        s_rawp = [sem(f"s_rawp{n}") for n in range(KB)]
        s_condb = sem("s_condb")
        s_w2raw = sem("s_w2raw")
        s_raw = [sem(f"s_raw{n}") for n in range(4)]
        s_c2 = sem("s_c2")
        s_zeros = sem("s_zeros")
        s_la = sem("s_la")
        s_lb = sem("s_lb")
        s_reshi = sem("s_reshi")
        s_reslo = sem("s_reslo")
        s_w2lo = sem("s_w2lo")
        s_w2hi = sem("s_w2hi")
        s_wf = sem("s_wf")
        s_wfu = sem("s_wfu")
        s_hlo = sem("s_hlo")
        s_t = sem("s_t")
        s_y = sem("s_y")
        s_out = [sem(f"s_out{n}") for n in range(HALVES)]
        s_const = sem("s_const")
        s_projhi = sem("s_projhi")
        s_cond = sem("s_cond")
        s_xchi = sem("s_xchi")
        s_rope = sem("s_rope")
        s_kmhi = sem("s_kmhi")
        s_projlo = sem("s_projlo")
        s_qhi = sem("s_qhi")
        s_proj = sem("s_proj")
        s_vT = sem("s_vT")
        s_on = sem("s_on")
        s_ahi = sem("s_ahi")
        s_ST = sem("s_ST")
        s_pused = sem("s_pused")
        s_exp = sem("s_exp")
        s_x1 = sem("s_x1")
        s_x1hi = sem("s_x1hi")
        s_xbhi = sem("s_xbhi")
        s_g = sem("s_g")
        s_th = sem("s_th")
        s_h = sem("s_h")
        s_hhi = sem("s_hhi")
        s_h1 = sem("s_h1")
        s_tgu = sem("s_tgu")
        s_sw = sem("s_sw")
        s_sin = sem("s_sin")
        s_cos = sem("s_cos")
        s_alo = sem("s_alo")
        s_p = sem("s_p")
        s_x1lo = sem("s_x1lo")
        s_init = sem("s_init")
        s_headrow = sem("s_headrow")
        s_xclo = sem("s_xclo")
        s_kmlo = sem("s_kmlo")
        s_qlo = sem("s_qlo")
        s_S = sem("s_S")
        s_max = sem("s_max")
        s_mT = sem("s_mT")
        s_shift = sem("s_shift")
        s_rec = sem("s_rec")
        s_vtr = sem("s_vtr")
        s_v = sem("s_v")
        s_wo = sem("s_wo")
        s_lh = sem("s_lh")
        s_lhs = sem("s_lhs")
        s_xblo = sem("s_xblo")
        s_zp = sem("s_zp")
        s_zhi = sem("s_zhi")
        s_z = sem("s_z")
        s_u = sem("s_u")
        s_dl = sem("s_dl")
        s_dno = sem("s_dno")

        block = ctx.enter_context(nc.Block())

        @block.sync
        def _(sp):
            def load_adapter(i, b):
                a = sp.value_load(ids_sb[0:1, i * NB + b:i * NB + b + 1], min_val=0, max_val=ADAPTERS - 1)
                sp.dma_start(adapter[b], cond_w[bass.ds(a, 1)].rearrange("a p n -> p (a n)")).then_inc(s_wc[b], 16)

            def load_x(i):
                sp.dma_start(xres[:, :, :], xT[i]).then_inc(s_x, 16)

            sp.dma_start(ids_sb[:, :], ids).then_inc(s_ids, 16)
            sp.wait_ge(s_ids, 16)
            for i in range(HALVES):
                if i == 0:
                    load_adapter(0, 0)
                    load_x(0)
                    for b in range(1, NB):
                        load_adapter(0, b)
                    for k in range(KB):
                        sp.dma_start(raw_proj[:, k, :], proj_w[:, PROJ * P * k:PROJ * P * (k + 1)]).then_inc(s_rawp[k], 16)
                sp.wait_ge(s_condb, i * NB + 1)
                sp.dma_start(stage_flat[:, 0:2048], c2_w).then_inc(s_w2raw, 16)
                if i == 0:
                    sp.wait_ge(s_condb, 2)
                    sp.dma_start(stage_flat[:, 2048:4096], wo_w).then_inc(s_raw[0], 16)
                if i:
                    sp.wait_ge(s_c2, i * KB)
                sp.wait_ge(s_zeros, 4)
                for b in range(NB):
                    a = sp.value_load(ids_sb[0:1, B + i * NB + b:B + i * NB + b + 1], min_val=0, max_val=SLOTS - 1)
                    sp.dma_start(loraA[:, b, :, :].rearrange("p k r -> p (k r)"),
                                 c2_A[bass.ds(a, 1)].rearrange("a p n -> p (a n)")).then_inc(s_la, 16)
                    sp.dma_start(loraB[32 * b:32 * b + R2, :],
                                 c2_B[bass.ds(a, 1)].rearrange("a r n -> r (a n)")).then_inc(s_lb, 16)
                if i == 0:
                    for r, parts in enumerate([[(0, gB), (IP, dB)], [(0, uB), (IP, dA)], [(0, gA), (512, uA)]]):
                        sp.wait_ge(s_reshi, (1, 3, 6)[r])
                        sp.wait_ge(s_reslo, (1, 3, 6)[r])
                        for at, src in parts:
                            sp.dma_start(stage_flat[:, 2048 + at:2048 + at + src.shape[1]],
                                         src).then_inc(s_raw[r + 1], 16)
                    sp.wait_ge(s_reshi, 7)
                    sp.wait_ge(s_reslo, 7)
                for m in range(W_CHUNKS):
                    s = wi(m)
                    if m < 2:
                        sp.wait_ge(s_condb, i * NB + 2)
                    elif m < 4:
                        sp.wait_ge(s_w2lo, i * KB + KB)
                        sp.wait_ge(s_w2hi, i * KB + KB)
                    else:
                        sp.wait_ge(s_wf, i * W_CHUNKS + m - 3)
                        sp.wait_ge(s_wfu, i * U_CHUNKS + m - 3)
                    n = 512 if m == W_CHUNKS - 1 and I_TILES % 2 else 1024
                    src = gu_q[m] if m < I_TILES else dn_q[m - I_TILES, :, 0:n]
                    sp.dma_start(stage[:, s, 0:n].bitcast(I32), src).then_inc(s_wi[s], 16)
                if i + 1 < HALVES:
                    sp.wait_ge(s_wf, (i + 1) * W_CHUNKS)
                    sp.wait_ge(s_wfu, (i + 1) * U_CHUNKS)
                    load_adapter(i + 1, 0)
                    load_adapter(i + 1, 1)
                    sp.wait_ge(s_hlo, (i + 1) * I_TILES)
                    sp.wait_ge(s_t, (i + 1) * KB)
                    load_x(i + 1)
                    load_adapter(i + 1, 2)
                for k in range(KB):
                    sp.wait_ge(s_y, i * KB + k + 1)
                    sp.dma_start(out[i, :, k], slots[:, k, :]).then_inc(s_out[i], 16)
                if i + 1 < HALVES:
                    sp.wait_ge(s_out[i], KB * 16)
                    load_adapter(i + 1, 3)
            for i in range(HALVES):
                sp.wait_ge(s_out[i], KB * 16)

        @block.scalar
        def _(act):
            for dst, src in ((rope[:, :, :], rope_tab), (maskq[:, :], causal), (eyef[:, :], eye),
                             (keyrow[:, :], key_rows), (headcol[:, :], head_cols), (scale[:, :], scales),
                             (bias2[:, :], c2_b)):
                act.dma_start(dst, src).then_inc(s_const, 16)

            def project_hi(k):
                act.wait_ge(s_rawp[k], 16)
                nc.scalar.activation(projw[:, 0, k, :], raw_proj[:, k, :], ACT.Copy).then_inc(s_projhi, 1)

            def resident_hi(r):
                act.wait_ge(s_raw[r], 16 if r == 0 else 32)
                if r == 0:
                    nc.scalar.activation(wow[:, 0, :, :], raw_wo, ACT.Copy).then_inc(s_reshi, 1)
                elif r == 1:
                    nc.scalar.activation(guB[:, 0, :], raw_B, ACT.Copy).then_inc(s_reshi, 1)
                    nc.scalar.activation(dnB[:, 0, :], raw_dB, ACT.Copy).then_inc(s_reshi, 1)
                elif r == 2:
                    nc.scalar.activation(guB[:, 1, :], raw_B, ACT.Copy).then_inc(s_reshi, 1)
                    for c in (0, 1):
                        nc.scalar.activation(dnA[:, :, c, :], raw_dA, ACT.Copy).then_inc(s_reshi, 1)
                else:
                    nc.scalar.activation(guA[:, 0, :, :, :], raw_guA, ACT.Copy).then_inc(s_reshi, 1)

            for i in range(HALVES):
                if i == 0:
                    project_hi(0)
                for k in range(KB):
                    act.wait_ge(s_cond, i * KB + k + 1)
                    nc.scalar.activation(xc[:, 0, k, :], bank[k][:, :], ACT.Copy).then_inc(s_xchi, 1)
                if i == 0:
                    for k in range(1, KB):
                        project_hi(k)
                    act.wait_ge(s_const, 16 * 7)
                for t in range(2):
                    act.wait_ge(s_rope, i * 6 + t + 1)
                    for g in range(4):
                        nc.scalar.activation(km[:, 0, 4 * t + g, :], slots[:, 2 + t, :], ACT.Copy,
                                             scale=keyrow[:, g:g + 1]).then_inc(s_kmhi, 1)
                for j in range(GROUPS):
                    act.wait_ge(s_rope, i * 6 + j + 3)
                    if i == 0 and j == 0:
                        act.wait_ge(s_projlo, KB)
                    nc.scalar.activation(qq[0:64, 0, j, :], slots[0:64, 4 + j, :], ACT.Copy).then_inc(s_qhi, 1)
                    nc.scalar.activation(qq[64:128, 1, j, :], slots[64:128, 4 + j, :], ACT.Copy).then_inc(s_qhi, 1)
                act.wait_ge(s_proj, i * PROJ + PROJ)
                nc.scalar.activation(nrm[:, 0, :], bank[2][:, :], ACT.Copy).then_inc(s_vT, 1)

                def attention_hi(b):
                    act.wait_ge(s_on, i * ON + b + 1)
                    nc.scalar.activation(att[:, 0, :, S * b:S * b + S],
                                         nrm[:, b % 2, :].rearrange("p (j n) -> p j n", j=GROUPS),
                                         ACT.Copy).then_inc(s_ahi, 1)

                for b in range(NB):
                    for n in range(NKV):
                        act.wait_ge(s_ST, i * 32 + 8 * b + n + 1)
                        if b:
                            act.wait_ge(s_pused, i * 8 + 2 * b - (1 if n < 4 else 0))
                        nc.scalar.activation(slots[:, n, :], bank[ST_BANK[(8 * b + n) % 3]][:, :], ACT.Exp,
                                             scale=QK_SCALE).then_inc(s_exp, 1)
                    if b:
                        attention_hi(b - 1)
                    if i == 0 and b < 3:
                        resident_hi(b)
                b = NB - 1
                for j in range(GROUPS):
                    act.wait_ge(s_on, i * ON + b + j + 1)
                    nc.scalar.activation(att[:, 0, j, S * b:S * b + S], nrm[:, b % 2, S * j:S * j + S],
                                         ACT.Copy).then_inc(s_ahi, 1)
                act.wait_ge(s_w2raw, i * 16 + 16)
                for k in range(KB):
                    nc.scalar.activation(w2[:, 0, k, :], raw_w2[:, k, :], ACT.Copy).then_inc(s_w2hi, 1)
                for k in range(KB):
                    act.wait_ge(s_x1, i * KB + k + 1)
                    nc.scalar.activation(x1[:, 0, k, :], xres[:, k, :], ACT.Copy).then_inc(s_x1hi, 1)
                if i == 0:
                    resident_hi(3)

                def convert(m):
                    if m == W_CHUNKS - 1 and I_TILES % 2:
                        return
                    wait_convert(act, i, m)
                    nc.scalar.activation(wf[:, m % 2, 512:1024], stage[:, wi(m), 512:1024].bitcast(I32), ACT.Copy,
                                         bias=-Q_ZERO).then_inc(s_wfu, 1)

                for k in range(KB):
                    act.wait_ge(s_c2, i * KB + k + 1)
                    nc.scalar.activation(xb[:, 0, k, :], bank[k][:, :], ACT.Identity,
                                         bias=bias2[:, k:k + 1]).then_inc(s_xbhi, 1)
                convert(0)
                convert(1)

                def tanh(n):
                    act.wait_ge(s_g, i * I_TILES + n + 1)
                    nc.scalar.activation(slots[:, 4 + n % 2, :], slots[:, n % 2, :], ACT.Tanh,
                                         scale=0.5).then_inc(s_th, 1)

                def hidden_hi(n):
                    act.wait_ge(s_h, i * I_TILES + n + 1)
                    nc.scalar.activation(hid(n, 0), slots[:, U_SLOT[n % 4], :], ACT.Copy).then_inc(s_hhi, 1)

                for n in range(I_TILES):
                    gate, up = bank[4 * (n % 2)], bank[4 * (n % 2) + 1]
                    convert(n + 2)
                    act.wait_ge(s_gu, i * I_TILES + n + 1)
                    if n >= 2:
                        act.wait_ge(s_h1, i * I_TILES + n - 1)
                    nc.scalar.activation(slots[:, n % 2, :], gate[:, :], ACT.Copy,
                                         scale=scale[:, n:n + 1]).then_inc(s_tgu, 1)
                    if n >= 4:
                        act.wait_ge(s_hlo, i * I_TILES + n - 3)
                    nc.scalar.activation(slots[:, U_SLOT[n % 4], :], up[:, :], ACT.Copy,
                                         scale=scale[:, I_TILES + n:I_TILES + n + 1]).then_inc(s_tgu, 1)
                    if n >= 1:
                        tanh(n - 1)
                    if n >= 2:
                        hidden_hi(n - 2)
                tanh(I_TILES - 1)
                hidden_hi(I_TILES - 2)
                hidden_hi(I_TILES - 1)
                for m in range(I_TILES + 2, W_CHUNKS):
                    convert(m)

        @block.gpsimd
        def _(pool):
            nc.gpsimd.memset(vpad[:, :, :, :], 0.0).then_inc(s_zeros, 1)
            nc.gpsimd.memset(ones2[:, :, :], 0.0).then_inc(s_zeros, 1)
            nc.gpsimd.memset(lorah[:, :], 0.0).then_inc(s_zeros, 1)
            nc.gpsimd.memset(loraB[:, :], 0.0).then_inc(s_zeros, 1)
            pool.wait_ge(s_zeros, 4)
            nc.gpsimd.memset(ones2[:, 0, 0:16], 1.0).then_inc(s_zeros, 1)
            nc.gpsimd.memset(ones2[:, 1, 16:32], 1.0).then_inc(s_zeros, 1)
            pool.wait_ge(s_const, 16 * 7)

            def resident_lo(r):
                sub = nc.gpsimd.tensor_tensor
                pool.wait_ge(s_reshi, (1, 3, 6, 7)[r])
                if r == 0:
                    sub(wow[:, 1, :, :], raw_wo, f(wow[:, 0, :, :]), ALU.subtract).then_inc(s_reslo, 1)
                elif r == 1:
                    pool.wait_ge(s_alo, 1)
                    sub(guB[64:128, 0, :], raw_B[64:128], f(guB[64:128, 0, :]), ALU.subtract).then_inc(s_reslo, 1)
                    pool.wait_ge(s_reslo, 2)
                    sub(dnB[:, 1, :], raw_dB, f(dnB[:, 0, :]), ALU.subtract).then_inc(s_reslo, 1)
                elif r == 2:
                    pool.wait_ge(s_alo, 2)
                    sub(guB[64:128, 1, :], raw_B[64:128], f(guB[64:128, 1, :]), ALU.subtract).then_inc(s_reslo, 1)
                    pool.wait_ge(s_reslo, 4)
                    for c in (2, 3):
                        sub(dnA[:, :, c, :], raw_dA, f(dnA[:, :, 0, :]), ALU.subtract).then_inc(s_reslo, 1)
                else:
                    sub(guA[:, 1, :, :, :], raw_guA, f(guA[:, 0, :, :, :]), ALU.subtract).then_inc(s_reslo, 1)

            for i in range(HALVES):
                for t in range(6):
                    pool.wait_ge(s_sw, i * 6 + t + 1)
                    sw = slots[:, t % 2, :].rearrange("p (b n) -> p b n", b=NB)
                    sin = rope[:, 1:2, :].broadcast_to([P, NB, S])
                    nc.gpsimd.tensor_tensor(sw, sw, sin, ALU.mult).then_inc(s_sin, 1)
                    pool.wait_ge(s_sin, i * 6 + t + 1)
                    pool.wait_ge(s_cos, i * 6 + t + 1)
                    nc.gpsimd.tensor_tensor(slots[:, 2 + t, :], slots[:, 2 + t, :], slots[:, t % 2, :],
                                            ALU.add).then_inc(s_rope, 1)

                def attention_lo(b):
                    pool.wait_ge(s_ahi, i * ON + b + 1)
                    nc.gpsimd.tensor_tensor(att[:, 1, :, S * b:S * b + S],
                                            nrm[:, b % 2, :].rearrange("p (j n) -> p j n", j=GROUPS),
                                            f(att[:, 0, :, S * b:S * b + S]), ALU.subtract).then_inc(s_alo, 1)

                for b in range(NB):
                    for n in range(NKV):
                        pool.wait_ge(s_exp, i * 32 + 8 * b + n + 1)
                        p = slots[:, n, :].rearrange("p (j q) -> p j q", j=GROUPS)
                        nc.gpsimd.affine_select(out=p, in_=p, compare_op=ALU.is_ge, fill=0.0, base=0,
                                                pattern=[[0, GROUPS], [1, S]],
                                                channel_multiplier=-1).then_inc(s_p, 1)
                    if b:
                        attention_lo(b - 1)
                    if i == 0 and b < 3:
                        resident_lo(b)
                b = NB - 1
                for j in range(GROUPS):
                    pool.wait_ge(s_ahi, i * ON + b + j + 1)
                    nc.gpsimd.tensor_tensor(att[:, 1, j, S * b:S * b + S], nrm[:, b % 2, S * j:S * j + S],
                                            f(att[:, 0, j, S * b:S * b + S]), ALU.subtract).then_inc(s_alo, 1)
                for k in range(KB):
                    pool.wait_ge(s_w2hi, i * KB + k + 1)
                    nc.gpsimd.tensor_tensor(w2[:, 1, k, :], raw_w2[:, k, :], f(w2[:, 0, k, :]),
                                            ALU.subtract).then_inc(s_w2lo, 1)
                for k in range(KB):
                    pool.wait_ge(s_x1hi, i * KB + k + 1)
                    nc.gpsimd.tensor_tensor(x1[:, 1, k, :], xres[:, k, :], f(x1[:, 0, k, :]),
                                            ALU.subtract).then_inc(s_x1lo, 1)
                if i == 0:
                    resident_lo(3)
                for n in range(I_TILES):
                    pool.wait_ge(s_hhi, i * I_TILES + n + 1)
                    nc.gpsimd.tensor_tensor(hid(n, 1), slots[:, U_SLOT[n % 4], :], f(hid(n, 0)),
                                            ALU.subtract).then_inc(s_hlo, 1)

        @block.vector
        def _(dve):
            dve.wait_ge(s_const, 16 * 7)
            nc.vector.tensor_scalar(scale[:, :], scale[:, :], Q_STEP, None, ALU.mult).then_inc(s_init, 1)
            nc.vector.tensor_copy(eyeb[:, :], eyef[:, :]).then_inc(s_init, 1)
            nc.vector.tensor_reduce(headrow[:, :], eyef[0:NH, 0:NH].rearrange("h (g j) -> h g j", j=GROUPS),
                                    AX_X, ALU.max).then_inc(s_headrow, 1)
            dve.wait_ge(s_headrow, 1)
            nc.vector.tensor_copy(headsel[:, :, :], headrow[:, :].rearrange("h (g o) -> h g o", o=1)
                                  .broadcast_to([NH, NKV, P])).then_inc(s_init, 1)

            def project_lo(k):
                dve.wait_ge(s_projhi, k + 1)
                nc.vector.tensor_tensor(projw[:, 1, k, :], raw_proj[:, k, :], f(projw[:, 0, k, :]),
                                        ALU.subtract).then_inc(s_projlo, 1)

            for i in range(HALVES):
                if i == 0:
                    project_lo(0)
                for k in range(KB):
                    dve.wait_ge(s_xchi, i * KB + k + 1)
                    nc.vector.tensor_tensor(xc[:, 1, k, :], bank[k][:, :], f(xc[:, 0, k, :]),
                                            ALU.subtract).then_inc(s_xclo, 1)
                if i == 0:
                    for k in range(1, KB):
                        project_lo(k)

                def rotate(t):
                    ps = bank[PROJ_BANK[t]]
                    dve.wait_ge(s_proj, i * PROJ + t + 1)
                    if t >= 2:
                        dve.wait_ge(s_rope, i * 6 + t - 1)
                    nc.vector.stream_shuffle(slots[:, t % 2, :], ps[:, :],
                                             [16 * (p // 16) + (p + 8) % 16 for p in range(32)]).then_inc(s_sw, 1)
                    cos = rope[:, 0:1, :].broadcast_to([P, NB, S])
                    nc.vector.tensor_tensor(slots[:, 2 + t, :].rearrange("p (b n) -> p b n", b=NB),
                                            ps[:, :].rearrange("p (b n) -> p b n", b=NB), cos,
                                            ALU.mult).then_inc(s_cos, 1)

                def k_lo(t):
                    for g in range(4):
                        dve.wait_ge(s_kmhi, i * 8 + 4 * t + g + 1)
                        nc.vector.scalar_tensor_tensor(out=km[:, 1, 4 * t + g, :], in0=slots[:, 2 + t, :],
                                                       scalar=keyrow[:, g:g + 1], in1=f(km[:, 0, 4 * t + g, :]),
                                                       op0=ALU.mult, op1=ALU.subtract).then_inc(s_kmlo, 1)

                def q_lo(j):
                    dve.wait_ge(s_qhi, i * 8 + 2 * j + 2)
                    nc.vector.tensor_tensor(qq[64:128, 0, j, :], slots[0:64, 4 + j, :], f(qq[0:64, 0, j, :]),
                                            ALU.subtract).then_inc(s_qlo, 1)
                    nc.vector.tensor_tensor(qq[0:64, 1, j, :], slots[64:128, 4 + j, :], f(qq[64:128, 1, j, :]),
                                            ALU.subtract).then_inc(s_qlo, 1)

                def maxima(s):
                    b, j, t = s // 8, s % 8 // 2, s % 2
                    dve.wait_ge(s_S, i * 32 + s + 1)
                    nc.vector.tensor_reduce(mx[:, b % 2, 4 * t:4 * t + 4, j],
                                            bank[4 + s % 2][:, :].rearrange("p (g k) -> p g k", g=4),
                                            AX_X, ALU.max).then_inc(s_max, 1)

                def store_shift(b):
                    dve.wait_ge(s_mT, i * NB + b + 1)
                    if b:
                        dve.wait_ge(s_ST, i * 32 + 8 * b)
                    mt = bank[2][0:NH, 0:S].rearrange("h (o q) -> h o q", o=1).broadcast_to([NH, GROUPS, S])
                    sel = headcol[:, :].rearrange("h (j o) -> h j o", o=1).broadcast_to([NH, GROUPS, S])
                    nc.vector.tensor_tensor(shift[:, :, :], mt, sel, ALU.mult).then_inc(s_shift, 1)

                def reciprocal(b, j):
                    if j == 0:
                        dve.wait_ge(s_pused, i * 8 + 2 * b + 2)
                        if b >= 2:
                            dve.wait_ge(s_alo, i * ON + b - 1)
                    nc.vector.reciprocal(nrm[:, b % 2, S * j:S * j + S], bank[1][:, S * j:S * j + S]).then_inc(s_rec, 1)

                def normalise(b):
                    dve.wait_ge(s_rec, i * 16 + 4 * b + 4)
                    nc.vector.tensor_tensor(nrm[:, b % 2, :], bank[0][:, :], nrm[:, b % 2, :],
                                            ALU.mult).then_inc(s_on, 1)

                rotate(0)
                rotate(1)
                rotate(2)
                k_lo(0)
                rotate(3)
                q_lo(0)
                rotate(4)
                q_lo(1)
                maxima(0)
                maxima(1)
                rotate(5)
                maxima(2)
                maxima(3)
                k_lo(1)
                q_lo(2)
                maxima(4)
                maxima(5)
                q_lo(3)
                maxima(6)
                maxima(7)
                dve.wait_ge(s_vtr, i + 1)
                vt = bank[3][:, :].rearrange("p (b m c d) -> p b m c d", b=NB, m=PAIRS, c=2)
                vp = vpad[:, :, :, :].rearrange("p b (m c) n -> p b m c n", c=2)
                for c in range(2):
                    nc.vector.tensor_copy(vp[:, :, :, c, 16 * c:16 * c + 16], vt[:, :, :, c, :]).then_inc(s_v, 1)
                store_shift(0)
                for s in range(8, 32):
                    b, n = s // 8, (s - LEAD) % 8
                    maxima(s)
                    if (s - LEAD) // 8 >= 1 and s >= LEAD:
                        if n < 4:
                            reciprocal((s - LEAD) // 8 - 1, n)
                        elif n == 4:
                            normalise((s - LEAD) // 8 - 1)
                    if s >= 16 and (s - LEAD) % 8 == 7:
                        store_shift((s - LEAD + 1) // 8)
                store_shift(NB - 1)
                for j in range(GROUPS):
                    reciprocal(NB - 2, j)
                normalise(NB - 2)
                b = NB - 1
                for j in range(GROUPS):
                    reciprocal(b, j)
                    dve.wait_ge(s_rec, i * 16 + 4 * b + j + 1)
                    nc.vector.tensor_tensor(nrm[:, b % 2, S * j:S * j + S], bank[0][:, S * j:S * j + S],
                                            nrm[:, b % 2, S * j:S * j + S], ALU.mult).then_inc(s_on, 1)
                for k in range(KB):
                    dve.wait_ge(s_wo, i * KB + k + 1)
                    nc.vector.tensor_tensor(xres[:, k, :], bank[4 + k][:, :], xres[:, k, :],
                                            ALU.add).then_inc(s_x1, 1)
                for b in range(NB):
                    dve.wait_ge(s_lh, i * NB + b + 1)
                    nc.vector.tensor_scalar(lorah[32 * b:32 * b + R2, S * b:S * b + S],
                                            bank[4][32 * b:32 * b + R2, 0:S], LORA_SCALE, None,
                                            ALU.mult).then_inc(s_lhs, 1)
                for k in range(KB):
                    dve.wait_ge(s_xbhi, i * KB + k + 1)
                    nc.vector.scalar_tensor_tensor(out=xb[:, 1, k, :], in0=bank[k][:, :], scalar=bias2[:, k:k + 1],
                                                   in1=f(xb[:, 0, k, :]), op0=ALU.add,
                                                   op1=ALU.subtract).then_inc(s_xblo, 1)

                def low_rank(k, w, ps):
                    dve.wait_ge(s_zp, i * 3 + k + 1)
                    nc.vector.tensor_copy(z[:, w, :], ps[:, :]).then_inc(s_zhi, 1)
                    dve.wait_ge(s_zhi, i * 3 + k + 1)
                    for r in (32, 96):
                        nc.vector.tensor_tensor(z[r:r + 32, w, :], ps[r:r + 32, :], f(z[r:r + 32, w, :]),
                                                ALU.subtract).then_inc(s_z, 1)

                def convert(m):
                    wait_convert(dve, i, m)
                    nc.vector.tensor_scalar(wf[:, m % 2, 0:512], stage[:, wi(m), 0:512].bitcast(I32), -Q_ZERO, None,
                                            ALU.add).then_inc(s_wf, 1)

                def hidden(n):
                    g, u, th = slots[:, n % 2, :], slots[:, U_SLOT[n % 4], :], slots[:, 4 + n % 2, :]
                    dve.wait_ge(s_th, i * I_TILES + n + 1)
                    nc.vector.scalar_tensor_tensor(out=th, in0=th, scalar=1.0, in1=g, op0=ALU.add,
                                                   op1=ALU.mult).then_inc(s_h1, 1)
                    dve.wait_ge(s_h1, i * I_TILES + n + 1)
                    dve.wait_ge(s_u, i * I_TILES + n + 1)
                    nc.vector.scalar_tensor_tensor(out=u, in0=th, scalar=0.5, in1=u, op0=ALU.mult,
                                                   op1=ALU.mult).then_inc(s_h, 1)

                convert(0)
                convert(1)
                low_rank(0, 0, bank[5])
                low_rank(1, 1, bank[6])
                for n in range(I_TILES):
                    gl, ul = bank[4 * (n % 2) + 2], bank[4 * (n % 2) + 3]
                    g, u = slots[:, n % 2, :], slots[:, U_SLOT[n % 4], :]
                    convert(n + 2)
                    dve.wait_ge(s_tgu, i * 2 * I_TILES + 2 * n + 1)
                    nc.vector.scalar_tensor_tensor(out=g, in0=gl[:, :], scalar=LR_SCALE, in1=g, op0=ALU.mult,
                                                   op1=ALU.add).then_inc(s_g, 1)
                    dve.wait_ge(s_tgu, i * 2 * I_TILES + 2 * n + 2)
                    nc.vector.scalar_tensor_tensor(out=u, in0=ul[:, :], scalar=LR_SCALE, in1=u, op0=ALU.mult,
                                                   op1=ALU.add).then_inc(s_u, 1)
                    if n:
                        hidden(n - 1)
                hidden(I_TILES - 1)
                for m in range(I_TILES + 2, I_TILES + 4):
                    convert(m)
                low_rank(2, 0, bank[0])
                for m in range(I_TILES + 4, W_CHUNKS):
                    convert(m)
                for k in range(KB):
                    dve.wait_ge(s_dl, i * KB + k + 1)
                    nc.vector.scalar_tensor_tensor(out=slots[:, k, :], in0=bank[k][:, :], scalar=LR_SCALE,
                                                   in1=xres[:, k, :], op0=ALU.mult, op1=ALU.add).then_inc(s_t, 1)
                for k in range(KB):
                    dve.wait_ge(s_t, i * KB + k + 1)
                    dve.wait_ge(s_dno, i * KB + k + 1)
                    nc.vector.scalar_tensor_tensor(out=slots[:, k, :], in0=bank[4 + k][:, :],
                                                   scalar=scale[:, 2 * I_TILES + k:2 * I_TILES + k + 1],
                                                   in1=slots[:, k, :], op0=ALU.mult, op1=ALU.add).then_inc(s_y, 1)

        @block.tensor
        def _(pe):
            mm = nc.tensor.matmul

            def split3(ps, whi, wlo, xhi, xlo, start, stop):
                mm(ps, whi, xhi, start=start, stop=False)
                mm(ps, whi, xlo, start=False, stop=False)
                return mm(ps, wlo, xhi, start=False, stop=stop)

            for i in range(HALVES):
                pe.wait_ge(s_x, i * 16 + 16)
                for b in range(NB):
                    pe.wait_ge(s_wc[b], i * 16 + 16)
                    w = adapter[b].rearrange("p (k n) -> p k n", k=KB)
                    for o in range(KB):
                        for k in range(KB):
                            last = mm(bank[o][:, S * b:S * b + S], w[:, k, P * o:P * o + P],
                                      xres[:, k, S * b:S * b + S], start=(k == 0), stop=(k == KB - 1))
                        if b == NB - 1:
                            last.then_inc(s_cond, 1)
                    if b < NB - 1:
                        last.then_inc(s_condb, 1)

                def project(t, k):
                    last = split3(bank[PROJ_BANK[t]][:, :], projw[:, 0, k, P * t:P * t + P],
                                  projw[:, 1, k, P * t:P * t + P], xc[:, 0, k, :], xc[:, 1, k, :],
                                  k == 0, k == KB - 1)
                    if k == KB - 1:
                        last.then_inc(s_proj, 1)

                if i:
                    pe.wait_ge(s_y, i * KB)
                for k in range(KB):
                    pe.wait_ge(s_xclo, i * KB + k + 1)
                    if i == 0:
                        pe.wait_ge(s_projlo, k + 1)
                    for t in range(2):
                        project(t, k)

                def scores(s):
                    b, j, t = s // 8, s % 8 // 2, s % 2
                    ps = bank[4 + s % 2]
                    if b == 0:
                        pe.wait_ge(s_kmhi, i * 8 + 4 * t + 4)
                        pe.wait_ge(s_qlo, i * 8 + 2 * j + 2)
                    if s >= 2:
                        pe.wait_ge(s_max, i * 32 + s - 1)
                    else:
                        pe.wait_ge(s_cos, i * 6 + 2)
                    mm(ps[:, :], eyeb[:, :], maskq[:, :], start=True, stop=False)
                    mm(ps[:, :], qq[:, t, j, S * b:S * b + S], km[:, 0, 4 * t:4 * t + 4, S * b:S * b + S],
                       start=False, stop=True).then_inc(s_S, 1)

                def turn_max(b):
                    pe.wait_ge(s_max, i * 32 + 8 * b + 8)
                    if b:
                        pe.wait_ge(s_shift, i * NB + b)
                    nc.tensor.transpose(bank[2][0:NH, 0:S], mx[:, b % 2, :, :].rearrange("p g j -> p (g j)"),
                                        eyef[:, :]).then_inc(s_mT, 1)

                def scores_turned(s):
                    b, g = s // 8, ST_ORDER[s % 8]
                    ps = bank[ST_BANK[s % 3]]
                    if s == 0:
                        pe.wait_ge(s_v, i * 2 + 2)
                        pe.wait_ge(s_kmlo, i * 8 + 8)
                    if s % 8 == 0:
                        pe.wait_ge(s_shift, i * NB + b + 1)
                    if s >= 3:
                        pe.wait_ge(s_exp, i * 32 + s - 2)
                    q = qq[:, g // 4, :, S * b:S * b + S]
                    mm(ps[:, :], km[:, 0, g, S * b:S * b + S], q, start=True, stop=False)
                    mm(ps[:, :], km[:, 1, g, S * b:S * b + S], q, start=False, stop=False)
                    mm(ps[:, :], headsel[:, g, :], shift[:, :, :].rearrange("h j q -> h (j q)"),
                       start=False, stop=True).then_inc(s_ST, 1)

                def values(b, c):
                    if c == 0 and b:
                        pe.wait_ge(s_on, i * ON + b)
                    pe.wait_ge(s_p, i * 32 + 8 * b + 4 * c + 4)
                    for m in range(PAIRS):
                        mm(bank[0][32 * m:32 * m + 32, :], vpad[:, b, 2 * m + c, :], slots[:, 4 * c + m, :],
                           start=(c == 0), stop=(c == 1), tile_position=(0, 32 * m))
                    for m in range(PAIRS):
                        last = mm(bank[1][32 * m:32 * m + 32, :], ones2[:, c, :], slots[:, 4 * c + m, :],
                                  start=(c == 0), stop=(c == 1), tile_position=(0, 32 * m))
                    last.then_inc(s_pused, 1)

                for t in range(2, 6):
                    for k in range(KB):
                        project(t, k)
                pe.wait_ge(s_init, 3)
                scores(0)
                scores(1)
                for k in range(KB):
                    project(6, k)
                for s in range(2, 4):
                    scores(s)
                pe.wait_ge(s_zeros, 6)
                scores(4)
                scores(5)
                pe.wait_ge(s_vT, i + 1)
                for b in range(NB):
                    last = nc.tensor.transpose(bank[3][:, S * b:S * b + S], nrm[:, 0, S * b:S * b + S], eyef[:, :])
                last.then_inc(s_vtr, 1)
                scores(6)
                scores(7)
                turn_max(0)
                for s in range(8, LEAD):
                    scores(s)
                for s in range(8 * NB):
                    scores_turned(s)
                    if s + LEAD < 8 * NB:
                        scores(s + LEAD)
                    if s % 8 == 7:
                        b = s // 8
                        if b + 1 < NB:
                            turn_max(b + 1)
                        values(b, 0)
                        values(b, 1)

                if i == 0:
                    pe.wait_ge(s_reslo, 1)
                for j in range(GROUPS):
                    pe.wait_ge(s_alo, i * ON + NB + j)
                    for o in range(KB):
                        last = split3(bank[4 + o][:, :], wow[:, 0, j, P * o:P * o + P], wow[:, 1, j, P * o:P * o + P],
                                      att[:, 0, j, :], att[:, 1, j, :], j == 0, j == GROUPS - 1)
                        if j == GROUPS - 1:
                            last.then_inc(s_wo, 1)
                pe.wait_ge(s_w2lo, i * KB + KB)
                for k in range(KB):
                    pe.wait_ge(s_x1lo, i * KB + k + 1)
                    if k == KB - 1:
                        pe.wait_ge(s_la, (i + 1) * 16 * NB)
                        for b in range(NB):
                            for kk in range(KB):
                                last = mm(bank[4][32 * b:32 * b + R2, 0:S], loraA[:, b, kk, :],
                                          xres[:, kk, S * b:S * b + S], start=(kk == 0), stop=(kk == KB - 1),
                                          tile_position=(0, 32 * b))
                            last.then_inc(s_lh, 1)
                    for o in range(KB):
                        split3(bank[o][:, :], w2[:, 0, k, P * o:P * o + P], w2[:, 1, k, P * o:P * o + P],
                               x1[:, 0, k, :], x1[:, 1, k, :], k == 0, False)
                pe.wait_ge(s_lb, (i + 1) * 16 * NB)
                pe.wait_ge(s_lhs, i * NB + NB)
                for o in range(KB):
                    mm(bank[o][:, :], loraB[:, P * o:P * o + P], lorah[:, :], start=False,
                       stop=True).then_inc(s_c2, 1)
                if i == 0:
                    pe.wait_ge(s_reslo, 7)
                for k in range(KB):
                    pe.wait_ge(s_xblo, i * KB + k + 1)
                    for w in range(2):
                        last = split3(bank[5 + w][:, :], guA[:, 0, w, k, :], guA[:, 1, w, k, :],
                                      xb[:, 0, k, :], xb[:, 1, k, :], k == 0, k == KB - 1)
                        if k == KB - 1:
                            last.then_inc(s_zp, 1)
                for n in range(I_TILES):
                    ps = [bank[4 * (n % 2) + c] for c in range(4)]
                    if n >= 2:
                        pe.wait_ge(s_u, i * I_TILES + n - 1)
                    pe.wait_ge(s_wf, i * W_CHUNKS + n + 1)
                    pe.wait_ge(s_wfu, i * U_CHUNKS + n + 1)
                    wt = wf[:, n % 2, :].rearrange("p (w k o) -> p w k o", w=2, k=KB)
                    for w in range(2):
                        for k in range(KB):
                            mm(ps[w][:, :], wt[:, w, k, :], xb[:, 0, k, :], start=(k == 0), stop=False)
                            mm(ps[w][:, :], wt[:, w, k, :], xb[:, 1, k, :], start=False, stop=(k == KB - 1))
                    if n == 0:
                        pe.wait_ge(s_z, i * 6 + 4)
                    for w in range(2):
                        last = mm(ps[2 + w][:, :], guB[:, w, P * n:P * n + P], z[:, w, :], start=True, stop=True)
                    last.then_inc(s_gu, 1)
                pe.wait_ge(s_u, i * I_TILES + I_TILES - 1)
                for c in range(D_CHUNKS):
                    m = I_TILES + c
                    if c == D_CHUNKS - 2:
                        pe.wait_ge(s_hlo, (i + 1) * I_TILES)
                        for n in range(I_TILES):
                            wt = dnA[:, n, :, :].rearrange("p c r -> p (c r)")
                            mm(bank[0][:, :], wt, hid(n, 0), start=(n == 0), stop=False)
                            last = mm(bank[0][:, :], wt, hid(n, 1), start=False, stop=(n == I_TILES - 1))
                        last.then_inc(s_zp, 1)
                    if c == D_CHUNKS - 1:
                        pe.wait_ge(s_z, i * 6 + 6)
                        for o in range(KB):
                            mm(bank[o][:, :], dnB[:, 0, P * o:P * o + P], z[:, 0, :], start=True, stop=False)
                            mm(bank[o][:, :], dnB[:, 1, P * o:P * o + P], z[:, 0, :], start=False,
                               stop=True).then_inc(s_dl, 1)
                    pe.wait_ge(s_wf, i * W_CHUNKS + m + 1)
                    pe.wait_ge(s_wfu, i * U_CHUNKS + min(m + 1, U_CHUNKS))
                    for n in range(2 * c, min(2 * c + 2, I_TILES)):
                        pe.wait_ge(s_hlo, i * I_TILES + n + 1)
                        for o in range(KB):
                            wt = wf[:, m % 2, 512 * (n % 2) + P * o:512 * (n % 2) + P * o + P]
                            mm(bank[4 + o][:, :], wt, hid(n, 0), start=(n == 0), stop=False)
                            last = mm(bank[4 + o][:, :], wt, hid(n, 1), start=False, stop=(n == I_TILES - 1))
                            if n == I_TILES - 1:
                                last.then_inc(s_dno, 1)
                    if c < D_CHUNKS - 1:
                        last.then_inc(s_dn, 1)


def kernel(**inputs):
    import numpy as np
    import ml_dtypes
    import concourse.bacc as bacc
    from concourse.bass_utils import run_bass_kernel_spmd

    a = {k: np.asarray(v) for k, v in inputs.items()}

    def blocks(w):
        return w.reshape(-1, P, w.shape[1]).transpose(1, 0, 2).reshape(P, -1)

    def pad(w, axis):
        n = IP - w.shape[axis]
        return np.pad(w, [(0, n if d == axis else 0) for d in range(w.ndim)])

    arrays = {}
    arrays["xT"] = a["x"].reshape(HALVES, T, KB, P).transpose(0, 3, 2, 1)
    arrays["ids"] = np.concatenate([a["itok_B_3_7"], a["itok_B_0_23"]]).reshape(1, 2 * B)
    arrays["cond_w"] = a["L0_cond_weight"].transpose(0, 2, 1).reshape(ADAPTERS, KB, P, H).transpose(
        0, 2, 1, 3).reshape(ADAPTERS, P, KB * H)
    wq = a["L0_attn_wq"].reshape(NKV, GROUPS, HD, H)
    wk = a["L0_attn_wk"].reshape(NKV, HD, H)
    rows = [np.tile(wk[4 * t:4 * t + 4].reshape(64, H), (2, 1)) for t in range(2)]
    rows += [wq[:, j].reshape(P, H) for j in range(GROUPS)] + [a["L0_attn_wv"]]
    arrays["proj_w"] = blocks(np.concatenate(rows).T)
    wo = a["L0_attn_wo"].T.reshape(NKV, GROUPS, HD, H).transpose(1, 0, 2, 3).reshape(H, H)
    arrays["wo_w"] = blocks(wo)
    arrays["c2_w"] = blocks(a["L0_cond2_W"].T)
    arrays["c2_b"] = a["L0_cond2_b"].reshape(KB, P).T
    arrays["c2_A"] = a["L0_cond2_lora_As"].reshape(SLOTS, KB, P, R2).transpose(0, 2, 1, 3).reshape(SLOTS, P, KB * R2)
    arrays["c2_B"] = a["L0_cond2_lora_Bs"]
    gu = np.stack([pad(a[f"L0_ffn_{n}_q"], 0) for n in ("gate", "up")])
    arrays["gu_q"] = gu.reshape(2, I_TILES, P, KB, P).transpose(1, 4, 0, 3, 2).reshape(I_TILES, P, 2 * KB * P)
    dn = pad(a["L0_ffn_down_q"].T, 0)
    dn = np.pad(dn, [(0, (2 * D_CHUNKS - I_TILES) * P), (0, 0)])
    arrays["dn_q"] = dn.reshape(D_CHUNKS, 2, P, H).transpose(0, 2, 1, 3).reshape(D_CHUNKS, P, 2 * H)
    arrays["scales"] = np.concatenate(
        [pad(a[f"L0_ffn_{n}_scale"], 0).reshape(I_TILES, P).T for n in ("gate", "up")]
        + [a["L0_ffn_down_scale"].reshape(KB, P).T], axis=1)
    arrays["gA"] = blocks(np.tile(a["L0_ffn_gate_A"], (1, 4)))
    arrays["uA"] = blocks(np.tile(a["L0_ffn_up_A"], (1, 4)))
    arrays["gB"] = np.tile(pad(a["L0_ffn_gate_B"], 1), (4, 1))
    arrays["uB"] = np.tile(pad(a["L0_ffn_up_B"], 1), (4, 1))
    arrays["dA"] = blocks(pad(a["L0_ffn_down_A"], 0))
    arrays["dB"] = np.tile(a["L0_ffn_down_B"], (4, 1))
    freq = (1.0 / np.float32(10000.0) ** (np.arange(0, HD, 2, dtype=np.float32) / np.float32(HD))).astype(np.float32)
    angle = np.arange(S, dtype=np.float32)[None, :] * np.concatenate([freq, freq])[:, None]
    sign = np.where(np.arange(HD) < HD // 2, -1.0, 1.0).astype(np.float32)[:, None]
    arrays["rope_tab"] = np.tile(np.stack([np.cos(angle), np.sin(angle) * sign], 1), (P // HD, 1, 1)).astype(np.float32)
    q, k = np.arange(S)[:, None], np.arange(S)[None, :]
    arrays["causal"] = np.tile(np.where(k <= q, 0.0, MASKED), (1, NB)).astype(ml_dtypes.bfloat16)
    arrays["eye"] = np.eye(P, dtype=np.float32)
    arrays["key_rows"] = (np.arange(P)[:, None] % 64 // HD == np.arange(4)).astype(np.float32)
    arrays["head_cols"] = -(np.arange(NH)[:, None] % GROUPS == np.arange(GROUPS)).astype(np.float32)

    nc = bacc.Bacc("TRN2", target_bir_lowering=False, num_devices=1)
    aps, ins = {}, {}
    for name, v in arrays.items():
        v = np.ascontiguousarray(v)
        ins[f"in_{name}_dram"] = v
        aps[name] = nc.dram_tensor(f"in_{name}_dram", v.shape, mybir.dt.from_np(v.dtype), kind="ExternalInput").ap()
    out = nc.dram_tensor("out_0_dram", (HALVES, P, KB, T), F32, kind="ExternalOutput").ap()
    adaln_attn_ffn(nc, out=out, **aps)
    r = run_bass_kernel_spmd(nc, [ins], core_ids=[0])
    got = r.results[0]["out_0_dram"]
    return np.ascontiguousarray(got.transpose(0, 3, 2, 1)).reshape(B, S, H)
```

```python
from contextlib import ExitStack

import concourse.bass as bass
from concourse import mybir

ALU = mybir.AluOpType
ACT = mybir.ActivationFunctionType
AX_X = mybir.AxisListType.X
F32 = mybir.dt.float32
F32R = mybir.dt.float32r
BF16 = mybir.dt.bfloat16
I32 = mybir.dt.int32

P = 128
H = 512
KB = H // P
B, S = 8, 128
HALVES = 2
NB = B // HALVES
T = NB * S
NH, NKV, HD = 32, 8, 16
GROUPS = NH // NKV
PAIRS = NKV // 2
QK_SCALE = HD ** -0.5
ADAPTERS, SLOTS, R2 = 8, 32, 16
R = 32
I_TILES = 11
IP = I_TILES * P
PROJ = 6
Q_ZERO, Q_STEP, LR_SCALE, LORA_SCALE = 7.5, 0.005, 0.02, 2.0
D_CHUNKS = (I_TILES + 1) // 2
W_CHUNKS = I_TILES + D_CHUNKS
U_CHUNKS = W_CHUNKS - I_TILES % 2
PROJ_BANK = (4, 5, 6, 7, 0, 2)
ROT = 1 + GROUPS
S_BANK = (4, 5, 3)
ST_BANK = (6, 7)
LATE = D_CHUNKS - 3
ORDER = [x for s in range(8 * NB) for x in [("scores", s)] + ([("max", s // 8 - 1)] if s > 8 and s % 8 == 1 else [])]
ORDER.append(("max", NB - 1))
FIRST = 11
LEAD = 13
ST_ORDER = [0, 2, 4, 6, 1, 3, 5, 7]
ON = NB - 1 + GROUPS
VALUES_AT = (0, 2)
SHIFT_AT = 6
EVACUATE_AT = 3
NORMALISE_AT = 1
SPLIT_AT = 2
KSEL_AT = (2, 4)
RECIPROCALS_AT = (28, 29, 30, 31)
MASKED = -1e30
WARM = (3, 2, 12, 3, 2, 10)


def adaln_attn_ffn(nc, xT, ids, cond_w, proj_w, wo_w, c2_w, c2_b, c2_A, c2_B, gu_q, dn_q, scales,
                   gA, uA, gB, uB, dA, dB, rope_tab, causal, eye, key_rows, head_cols, out):
    with ExitStack() as ctx:
        def sb(name, shape, dt):
            return ctx.enter_context(nc.sbuf_tensor(name, shape, dt))

        def sem(name):
            return ctx.enter_context(nc.semaphore(name))

        bank = [ctx.enter_context(nc.psum_tensor(f"bank{k}", [P, T], F32)) for k in range(8)]

        projw = sb("projw", [P, 2, KB, PROJ * P], F32R)
        wow = sb("wow", [P, 2, KB, H], F32R)
        guA = sb("guA", [P, 2, KB, 4, R], F32R)
        guB = sb("guB", [P, 2, IP], F32R)
        dnA = sb("dnA", [P, I_TILES, 4, R], F32R)
        dnB = sb("dnB", [P, H], F32R)
        headsel = sb("headsel", [NH, NKV, P], F32R)
        rope = sb("rope", [P, 2, S], F32)
        maskq = sb("maskq", [P, NB * S], BF16)
        eyef = sb("eyef", [P, P], F32)
        eyeb = sb("eyeb", [P, P], BF16)
        keyrow = sb("keyrow", [P, 5], F32)
        headcol = sb("headcol", [NH, GROUPS], F32)
        headrow = sb("headrow", [NH, NKV], F32)
        ones2 = sb("ones2", [P, 2, 32], F32)
        scale = sb("scale", [P, 2 * I_TILES + KB], F32)
        bias2 = sb("bias2", [P, KB], F32)
        ids_sb = sb("ids_sb", [1, 2 * B], I32)
        xres = sb("xres", [P, KB, T], F32)
        with nc.sbuf_tensor("qlm0", [P, GROUPS, T], F32R) as qlm0:
            pass
        stage = sb("stage", [P, 4, 1024], F32)
        wf = sb("wf", [P, 2, 1024], F32R)
        vpad = sb("vpad", [P, NB, NKV, 32], F32)
        slots = sb("slots", [P, 8, T], F32)
        nrm = sb("nrm", [P, 2, T], F32)
        pv = sb("pv", [P, T], F32)
        khi = sb("khi", [P, 2, T], F32R)
        mx = sb("mx", [P, 2, NKV, GROUPS], F32)
        loraA = sb("loraA", [P, NB, KB, 2 * R2], F32)
        loraB = sb("loraB", [P, H], F32)
        loraBp = sb("loraBp", [P, 2, H], F32R)
        lorah = sb("lorah", [P, T], F32R)
        xc = sb("xc", [P, 2, KB, T], F32R)
        with nc.sbuf_tensor("raw", [P, 8192], F32) as raw:
            pass
        raw_proj = raw[:, 0:KB * PROJ * P].rearrange("p (k n) -> p k n", k=KB)
        arena = sb("arena", [P, 3 * 4096], F32R)

        att = xc
        qhh = arena[:, 0:4096].rearrange("p (t j n) -> p t j n", t=2, j=GROUPS)
        x1 = arena[:, 0:4096].rearrange("p (a k n) -> p a k n", a=2, k=KB)
        khl = arena[:, 4096:8192].rearrange("p (g n) -> p g n", g=NKV)
        ksel = arena[:, 8192:12288].rearrange("p (g n) -> p g n", g=NKV)
        xb = arena[:, 4096:8192].rearrange("p (a k n) -> p a k n", a=2, k=KB)
        w2 = arena[:, 8192:12288].rearrange("p (a k n) -> p a k n", a=2, k=KB)
        z = arena[:, 11264:12288].rearrange("p (w n) -> p w n", w=2)
        xcf = xc[:, :, :, :].rearrange("p a k n -> p (a k n)")
        stage_flat = stage[:, :, :].rearrange("p a n -> p (a n)")
        slots_flat = slots[:, :, :].rearrange("p a n -> p (a n)")
        places = [stage_flat[:, 0:2048], stage_flat[:, 2048:4096], raw[:, 4096:6144], raw[:, 6144:8192]]
        adapter = [places, places[2:] + places[:2]]
        raw_w2 = stage_flat[:, 0:2048].rearrange("p (k n) -> p k n", k=KB)
        raw_wo = stage_flat[:, 2048:4096].rearrange("p (k n) -> p k n", k=KB)
        raw_B = stage_flat[:, 2048:2048 + IP]
        raw_dB = stage_flat[:, 2048 + IP:2048 + IP + H]
        raw_dA = stage_flat[:, 2048 + IP:2048 + IP + I_TILES * R].rearrange("p (n r) -> p n r", r=R)
        raw_guA = stage_flat[:, 2048:3072].rearrange("p (w k c r) -> p w k c r", w=2, k=KB, c=4)
        U_SLOT = (2, 3, 6, 7)

        R_SLOT = (2, 4, 5, 6, 7)
        kdup = (slots[:, 3, :], nrm[:, 1, :])
        qlm = (qlm0[:, :, :], wf[:, :, :].rearrange("p a n -> p (a n)").rearrange("p (j n) -> p j n", j=GROUPS))

        def hid(n, part):
            if n < 4:
                return xcf[:, 1024 * n + 512 * part:1024 * n + 512 * part + 512]
            at = (1024 * (n - 4) if n < 8 else 8192 + 1024 * (n - 8)) + 512 * part
            return arena[:, at:at + 512]

        def f(ap):
            return ap.bitcast(F32)

        def wi(m):
            return (m + 2) % 4

        wi_uses = [len([m for m in range(W_CHUNKS) if wi(m) == s]) for s in range(4)]

        def wait_convert(eng, i, m):
            s = wi(m)
            eng.wait_ge(s_wi[s], 16 * (i * wi_uses[s] + m // 4 + 1))
            if 2 <= m < I_TILES + 2:
                eng.wait_ge(s_gu, i * I_TILES + m - 1)
            elif m >= I_TILES + 2:
                eng.wait_ge(s_dn, i * D_CHUNKS + m - I_TILES - 1)

        s_wi = [sem(f"s_wi{n}") for n in range(4)]
        s_gu = sem("s_gu")
        s_dn = sem("s_dn")
        s_wc = [sem(f"s_wc{n}") for n in range(NB)]
        s_x = [sem(f"s_xin{n}") for n in range(NB)]
        s_ids = sem("s_ids")
        s_rawp = [sem(f"s_rawp{n}") for n in range(KB)]
        s_condb = sem("s_condb")
        s_w2raw = sem("s_w2raw")
        s_raw = [sem(f"s_raw{n}") for n in range(4)]
        s_c2 = sem("s_c2")
        s_zeros = sem("s_zeros")
        s_la = sem("s_la")
        s_lb = sem("s_lb")
        s_reshi = sem("s_reshi")
        s_reslo = sem("s_reslo")
        s_wolo = sem("s_wolo")
        s_w2lo = sem("s_w2lo")
        s_w2hi = sem("s_w2hi")
        s_wf = sem("s_wf")
        s_wfu = sem("s_wfu")
        s_hlo = sem("s_hlo")
        s_t = sem("s_t")
        s_y = sem("s_y")
        s_out = [sem(f"s_out{n}") for n in range(HALVES)]
        s_const = sem("s_const")
        s_projhi = sem("s_projhi")
        s_cond = sem("s_cond")
        s_xchi = sem("s_xchi")
        s_rope = sem("s_rope")
        s_kdup = [sem(f"s_kdup{n}") for n in range(2)]
        s_km = sem("s_km")
        s_sel = sem("s_sel")
        s_ksel = [sem(f"s_ksel{n}") for n in range(2)]
        s_ksin = sem("s_ksin")
        s_krope = sem("s_krope")
        s_projlo = sem("s_projlo")
        s_qhi = sem("s_qhi")
        s_proj = sem("s_proj")
        s_vT = sem("s_vT")
        s_on = sem("s_on")
        s_onlast = sem("s_onlast")
        s_ahi = sem("s_ahi")
        s_ST = sem("s_ST")
        s_pused = sem("s_pused")
        s_exp = sem("s_exp")
        s_x1 = sem("s_x1")
        s_x1hi = sem("s_x1hi")
        s_xbhi = sem("s_xbhi")
        s_g = sem("s_g")
        s_th = sem("s_th")
        s_h = sem("s_h")
        s_hhi = sem("s_hhi")
        s_h1 = sem("s_h1")
        s_tgu = sem("s_tgu")
        s_sw = sem("s_sw")
        s_sin = sem("s_sin")
        s_cos = sem("s_cos")
        s_alo = sem("s_alo")
        s_p = sem("s_p")
        s_x1lo = sem("s_x1lo")
        s_init = sem("s_init")
        s_headrow = sem("s_headrow")
        s_xclo = sem("s_xclo")
        s_khi = sem("s_khi")
        s_klo = sem("s_klo")
        s_qlo = sem("s_qlo")
        s_S = sem("s_S")
        s_max = sem("s_max")
        s_mT = sem("s_mT")
        s_shift = sem("s_shift")
        s_shift2 = sem("s_shift2")
        s_pv = sem("s_pv")
        s_rec = sem("s_rec")
        s_vtr = sem("s_vtr")
        s_v = sem("s_v")
        s_wo = sem("s_wo")
        s_lh = sem("s_lh")
        s_lhhi = sem("s_lhhi")
        s_lhs = sem("s_lhs")
        s_lzero = sem("s_lzero")
        s_lbhi = sem("s_lbhi")
        s_lblo = sem("s_lblo")
        s_xblo = sem("s_xblo")
        s_zp = sem("s_zp")
        s_zhi = sem("s_zhi")
        s_z = sem("s_z")
        s_u = sem("s_u")
        s_dl = sem("s_dl")
        s_dno = sem("s_dno")

        block = ctx.enter_context(nc.Block())

        @block.sync
        def _(sp):
            def load_adapter(i, b):
                a = sp.value_load(ids_sb[0:1, i * NB + b:i * NB + b + 1], min_val=0, max_val=ADAPTERS - 1)
                sp.dma_start(adapter[i][b], cond_w[bass.ds(a, 1)].rearrange("a p n -> p (a n)")).then_inc(s_wc[b], 16)

            def load_x(i, b):
                sp.dma_start(xres[:, :, S * b:S * b + S], xT[i, :, :, S * b:S * b + S]).then_inc(s_x[b], 16)

            sp.dma_start(ids_sb[:, :], ids).then_inc(s_ids, 16)
            load_x(0, 0)
            sp.wait_ge(s_ids, 16)
            for i in range(HALVES):
                if i == 0:
                    for b in range(NB):
                        load_adapter(0, b)
                        if b + 1 < NB:
                            load_x(0, b + 1)
                    for k in range(KB):
                        sp.dma_start(raw_proj[:, k, :], proj_w[:, PROJ * P * k:PROJ * P * (k + 1)]).then_inc(s_rawp[k], 16)
                if i == 0:
                    sp.wait_ge(s_condb, 2)
                    sp.dma_start(stage_flat[:, 2048:4096], wo_w).then_inc(s_raw[0], 16)
                sp.wait_ge(s_krope, i + 1)
                for t in range(2):
                    for r in range(2):
                        sp.dma_start(kdup[t][64 * r:64 * r + 64, :],
                                     slots[64 * t:64 * t + 64, 2, :]).then_inc(s_kdup[t], 16)
                if i:
                    sp.wait_ge(s_c2, i * KB)
                for b in range(NB):
                    a = sp.value_load(ids_sb[0:1, B + i * NB + b:B + i * NB + b + 1], min_val=0, max_val=SLOTS - 1)
                    sp.dma_start(loraA[:, b, :, :].rearrange("p k r -> p (k r)"),
                                 c2_A[bass.ds(a, 1)].rearrange("a p n -> p (a n)")).then_inc(s_la, 16)
                    sp.dma_start(loraB[32 * b:32 * b + 32, :],
                                 c2_B[bass.ds(a, 1)].rearrange("a r n -> r (a n)")).then_inc(s_lb, 16)
                def load_w2():
                    sp.wait_ge(s_ST, (i + 1) * 8 * NB)
                    sp.dma_start(stage_flat[:, 0:2048], c2_w).then_inc(s_w2raw, 16)

                if i:
                    load_w2()
                else:
                    for r, parts in enumerate([[(0, gB), (IP, dB)], [(0, uB), (IP, dA)], [(0, gA), (512, uA)]]):
                        sp.wait_ge(s_reshi, (1, 3, 7)[r])
                        if r:
                            sp.wait_ge(s_reslo, 2 * r)
                        else:
                            sp.wait_ge(s_wolo, 1)
                        for at, src in parts:
                            sp.dma_start(stage_flat[:, 2048 + at:2048 + at + src.shape[1]],
                                         src).then_inc(s_raw[r + 1], 16)
                        if r == 0:
                            load_w2()
                    sp.wait_ge(s_reshi, 8)
                    sp.wait_ge(s_reslo, 5)
                for m in range(W_CHUNKS):
                    s = wi(m)
                    if m < 2:
                        sp.wait_ge(s_cond, i * KB + KB)
                    elif m < 4:
                        sp.wait_ge(s_w2lo, i * KB + KB)
                        sp.wait_ge(s_w2hi, i * KB + KB)
                    else:
                        sp.wait_ge(s_wf, i * W_CHUNKS + m - 3)
                        sp.wait_ge(s_wfu, i * U_CHUNKS + m - 3)
                    n = 512 if m == W_CHUNKS - 1 and I_TILES % 2 else 1024
                    src = gu_q[m] if m < I_TILES else dn_q[m - I_TILES, :, 0:n]
                    sp.dma_start(stage[:, s, 0:n].bitcast(I32), src).then_inc(s_wi[s], 16)
                if i + 1 < HALVES:
                    sp.wait_ge(s_gu, (i + 1) * I_TILES)
                    load_adapter(i + 1, 0)
                    load_adapter(i + 1, 1)
                    sp.wait_ge(s_t, (i + 1) * KB)
                    for b in range(NB):
                        load_x(i + 1, b)
                    sp.wait_ge(s_wf, (i + 1) * W_CHUNKS)
                    sp.wait_ge(s_wfu, (i + 1) * U_CHUNKS)
                    load_adapter(i + 1, 2)
                    load_adapter(i + 1, 3)
                for k in range(KB):
                    sp.wait_ge(s_y, i * KB + k + 1)
                    sp.dma_start(out[i, :, k], slots[:, k, :]).then_inc(s_out[i], 16)
            for i in range(HALVES):
                sp.wait_ge(s_out[i], KB * 16)

        @block.scalar
        def _(act):
            for dst, src in ((rope[:, :, :], rope_tab), (maskq[:, :], causal), (eyef[:, :], eye),
                             (keyrow[:, :], key_rows), (headcol[:, :], head_cols), (scale[:, :], scales),
                             (bias2[:, :], c2_b)):
                act.dma_start(dst, src).then_inc(s_const, 16)

            def project_hi(k):
                act.wait_ge(s_rawp[k], 16)
                nc.scalar.activation(projw[:, 0, k, :], raw_proj[:, k, :], ACT.Copy).then_inc(s_projhi, 1)

            def resident_hi(r):
                act.wait_ge(s_raw[r], 16 if r == 0 else 32)
                if r == 0:
                    nc.scalar.activation(wow[:, 0, :, :], raw_wo, ACT.Copy).then_inc(s_reshi, 1)
                elif r == 1:
                    nc.scalar.activation(guB[:, 0, :], raw_B, ACT.Copy).then_inc(s_reshi, 1)
                    nc.scalar.activation(dnB[:, :], raw_dB, ACT.Copy).then_inc(s_reshi, 1)
                elif r == 2:
                    nc.scalar.activation(guB[:, 1, :], raw_B, ACT.Copy).then_inc(s_reshi, 1)
                    for c in (0, 1, 3):
                        nc.scalar.activation(dnA[:, :, c, :], raw_dA, ACT.Copy).then_inc(s_reshi, 1)
                else:
                    nc.scalar.activation(guA[:, :, :, :, :], raw_guA, ACT.Copy).then_inc(s_reshi, 1)

            act.wait_ge(s_zeros, 1)
            nc.scalar.activation(lorah[:, :], vpad[:, :, :, :].rearrange("p b g n -> p (b g n)")[:, 0:T],
                                 ACT.Copy).then_inc(s_lzero, 1)

            for i in range(HALVES):
                if i == 0:
                    project_hi(0)
                for k in range(KB):
                    act.wait_ge(s_cond, i * KB + k + 1)
                    nc.scalar.activation(xc[:, 0, k, :], bank[k][:, :], ACT.Copy).then_inc(s_xchi, 1)
                if i == 0:
                    for k in range(1, KB):
                        project_hi(k)
                    resident_hi(0)
                    act.wait_ge(s_const, 16 * 7)

                def k_hi(t):
                    act.wait_ge(s_kdup[t], 32 * (i + 1))
                    nc.scalar.activation(khi[64:128, t, :], kdup[t][64:128, :], ACT.Copy).then_inc(s_khi, 1)

                def k_masked(t):
                    act.wait_ge(s_klo, i * 2 + t + 1)
                    for g in range(4):
                        nc.scalar.activation(khl[:, 4 * t + g, :], kdup[t], ACT.Copy,
                                             scale=keyrow[:, g:g + 1]).then_inc(s_km, 1)

                def q_hi(j):
                    act.wait_ge(s_rope, i * GROUPS + j + 1)
                    if i == 0 and j == 0:
                        act.wait_ge(s_projlo, KB)
                    for t in range(2):
                        for r in (t, 1 - t):
                            nc.scalar.activation(qhh[64 * r:64 * r + 64, t, j, :], slots[64 * t:64 * t + 64, 4 + j, :],
                                                 ACT.Copy).then_inc(s_qhi, 1)

                k_hi(0)
                k_hi(1)
                k_masked(0)
                q_hi(0)
                k_masked(1)
                act.wait_ge(s_proj, i * PROJ + PROJ)
                nc.scalar.activation(nrm[:, 0, :], bank[PROJ_BANK[-1]][:, :], ACT.Copy).then_inc(s_vT, 1)
                for j in range(1, GROUPS):
                    q_hi(j)

                def copy_shift(b):
                    act.wait_ge(s_shift, i * NB + b + 1)
                    nc.scalar.activation(qlm[1][64:64 + NH, :, S * b:S * b + S],
                                         f(qlm[0][64:64 + NH, :, S * b:S * b + S]), ACT.Copy).then_inc(s_shift2, 1)

                def evacuate(b):
                    act.wait_ge(s_pused, i * 8 + 2 * b + 2)
                    if b:
                        act.wait_ge(s_on, i * (NB - 1) + b)
                    nc.scalar.activation(pv[:, :], bank[0][:, :], ACT.Copy).then_inc(s_pv, 1)

                def attention_hi(b):
                    act.wait_ge(s_on, i * (NB - 1) + b + 1)
                    nc.scalar.activation(att[:, 0, :, S * b:S * b + S],
                                         nrm[:, b % 2, :].rearrange("p (j n) -> p j n", j=GROUPS),
                                         ACT.Copy).then_inc(s_ahi, 1)

                copy_shift(0)
                for b in range(NB):
                    for n in range(NKV):
                        if b and n == EVACUATE_AT:
                            evacuate(b - 1)
                        if b > 1 and n == SPLIT_AT:
                            attention_hi(b - 2)
                        act.wait_ge(s_ST, i * 32 + 8 * b + n + 1)
                        if b:
                            act.wait_ge(s_pused, i * 8 + 2 * b - (1 if n < 4 else 0))
                        nc.scalar.activation(slots[:, n, :], bank[ST_BANK[n % 2]][:, :], ACT.Exp,
                                             scale=QK_SCALE).then_inc(s_exp, 1)
                        if n == SHIFT_AT and b + 1 < NB:
                            copy_shift(b + 1)
                attention_hi(NB - 2)
                b = NB - 1
                for j in range(GROUPS):
                    act.wait_ge(s_onlast, i * GROUPS + j + 1)
                    nc.scalar.activation(att[:, 0, j, S * b:S * b + S], nrm[:, b % 2, S * j:S * j + S],
                                         ACT.Copy).then_inc(s_ahi, 1)
                if i == 0:
                    resident_hi(1)
                act.wait_ge(s_w2raw, i * 16 + 16)
                for k in range(KB):
                    nc.scalar.activation(w2[:, 0, k, :], raw_w2[:, k, :], ACT.Copy).then_inc(s_w2hi, 1)
                act.wait_ge(s_lb, (i + 1) * 16 * NB)
                nc.scalar.activation(loraBp[:, 0, :], loraB[:, :], ACT.Copy, scale=LORA_SCALE).then_inc(s_lbhi, 1)
                for k in range(KB):
                    act.wait_ge(s_x1, i * KB + k + 1)
                    nc.scalar.activation(x1[:, 0, k, :], xres[:, k, :], ACT.Copy).then_inc(s_x1hi, 1)
                if i == 0:
                    resident_hi(2)
                    resident_hi(3)

                def convert(m):
                    if m == W_CHUNKS - 1 and I_TILES % 2:
                        return
                    wait_convert(act, i, m)
                    nc.scalar.activation(wf[:, m % 2, 512:1024], stage[:, wi(m), 512:1024].bitcast(I32), ACT.Copy,
                                         bias=-Q_ZERO).then_inc(s_wfu, 1)

                for k in range(KB):
                    act.wait_ge(s_c2, i * KB + k + 1)
                    nc.scalar.activation(xb[:, 0, k, :], bank[k][:, :], ACT.Identity,
                                         bias=bias2[:, k:k + 1]).then_inc(s_xbhi, 1)
                convert(0)
                convert(1)

                def tanh(n):
                    act.wait_ge(s_g, i * I_TILES + n + 1)
                    nc.scalar.activation(slots[:, 4 + n % 2, :], slots[:, n % 2, :], ACT.Tanh,
                                         scale=0.5).then_inc(s_th, 1)

                def hidden_hi(n):
                    act.wait_ge(s_h, i * I_TILES + n + 1)
                    nc.scalar.activation(hid(n, 0), slots[:, U_SLOT[n % 4], :], ACT.Copy).then_inc(s_hhi, 1)

                for n in range(I_TILES):
                    gate, up = bank[4 * (n % 2)], bank[4 * (n % 2) + 1]
                    convert(n + 2)
                    act.wait_ge(s_gu, i * I_TILES + n + 1)
                    if n >= 2:
                        act.wait_ge(s_h1, i * I_TILES + n - 1)
                    nc.scalar.activation(slots[:, n % 2, :], gate[:, :], ACT.Copy,
                                         scale=scale[:, n:n + 1]).then_inc(s_tgu, 1)
                    if n >= 4:
                        act.wait_ge(s_hlo, i * I_TILES + n - 3)
                    nc.scalar.activation(slots[:, U_SLOT[n % 4], :], up[:, :], ACT.Copy,
                                         scale=scale[:, I_TILES + n:I_TILES + n + 1]).then_inc(s_tgu, 1)
                    if n >= 1:
                        tanh(n - 1)
                    if n >= 2:
                        hidden_hi(n - 2)
                tanh(I_TILES - 1)
                hidden_hi(I_TILES - 2)
                hidden_hi(I_TILES - 1)
                for m in range(I_TILES + 2, W_CHUNKS):
                    convert(m)

        @block.gpsimd
        def _(pool):
            nc.gpsimd.memset(vpad[:, :, :, :], 0.0).then_inc(s_zeros, 1)
            nc.gpsimd.memset(ones2[:, :, :], 0.0).then_inc(s_zeros, 1)
            pool.wait_ge(s_zeros, 2)
            nc.gpsimd.memset(ones2[:, 0, 0:16], 1.0).then_inc(s_zeros, 1)
            nc.gpsimd.memset(ones2[:, 1, 16:32], 1.0).then_inc(s_zeros, 1)
            pool.wait_ge(s_const, 16 * 7)

            pool.wait_ge(s_reshi, 1)
            nc.gpsimd.tensor_tensor(wow[:, 1, :, :], raw_wo, f(wow[:, 0, :, :]), ALU.subtract).then_inc(s_wolo, 1)

            for i in range(HALVES):
                def rotate(t):
                    x, sw = slots[:, R_SLOT[t], :], slots[:, t % 2, :]
                    pool.wait_ge(s_sw, i * ROT + t + 1)
                    sw3 = sw.rearrange("p (b n) -> p b n", b=NB)
                    sin = rope[:, 1:2, :].broadcast_to([P, NB, S])
                    nc.gpsimd.tensor_tensor(sw3, sw3, sin, ALU.mult).then_inc(s_sin, 1)
                    pool.wait_ge(s_sin, i * GROUPS + t)
                    pool.wait_ge(s_cos, i * ROT + t + 1)
                    nc.gpsimd.tensor_tensor(x, x, sw, ALU.add).then_inc(s_rope, 1)

                pool.wait_ge(s_init, 3)
                if i:
                    pool.wait_ge(s_dno, i * KB)
                for b in range(NB):
                    pool.dma_start(ksel[64:64 + NH, :, S * b:S * b + S], headsel[:, :, :]).then_inc(s_sel, 16)
                for t in range(1, ROT):
                    rotate(t)
                    if t in KSEL_AT:
                        c = KSEL_AT.index(t)
                        pool.wait_ge(s_km, i * 8 + 4 * c + 4)
                        pool.dma_start(ksel[0:64, 4 * c:4 * c + 4, :],
                                       khl[0:64, 4 * c:4 * c + 4, :]).then_inc(s_ksel[c], 16)

                def normalise(b):
                    pool.wait_ge(s_pv, i * (NB - 1) + b + 1)
                    pool.wait_ge(s_rec, i * 16 + 4 * b + 4)
                    nc.gpsimd.tensor_tensor(nrm[:, b % 2, :], pv[:, :], nrm[:, b % 2, :], ALU.mult).then_inc(s_on, 1)

                def attention_lo(b):
                    pool.wait_ge(s_ahi, i * ON + b + 1)
                    nc.gpsimd.tensor_tensor(att[:, 1, :, S * b:S * b + S],
                                            nrm[:, b % 2, :].rearrange("p (j n) -> p j n", j=GROUPS),
                                            f(att[:, 0, :, S * b:S * b + S]), ALU.subtract).then_inc(s_alo, 1)

                for b in range(NB):
                    for n in range(NKV):
                        if b > 1 and n == NORMALISE_AT:
                            normalise(b - 2)
                        if b > 1 and n == SPLIT_AT + 1:
                            attention_lo(b - 2)
                        pool.wait_ge(s_exp, i * 32 + 8 * b + n + 1)
                        p = slots[:, n, :].rearrange("p (j q) -> p j q", j=GROUPS)
                        nc.gpsimd.affine_select(out=p, in_=p, compare_op=ALU.is_ge, fill=0.0, base=0,
                                                pattern=[[0, GROUPS], [1, S]],
                                                channel_multiplier=-1).then_inc(s_p, 1)
                normalise(NB - 2)
                attention_lo(NB - 2)
                b = NB - 1
                for j in range(GROUPS):
                    pool.wait_ge(s_ahi, i * ON + b + j + 1)
                    nc.gpsimd.tensor_tensor(att[:, 1, j, S * b:S * b + S], nrm[:, b % 2, S * j:S * j + S],
                                            f(att[:, 0, j, S * b:S * b + S]), ALU.subtract).then_inc(s_alo, 1)
                for k in range(KB):
                    pool.wait_ge(s_w2hi, i * KB + k + 1)
                    nc.gpsimd.tensor_tensor(w2[:, 1, k, :], raw_w2[:, k, :], f(w2[:, 0, k, :]),
                                            ALU.subtract).then_inc(s_w2lo, 1)
                for k in range(KB):
                    pool.wait_ge(s_x1hi, i * KB + k + 1)
                    nc.gpsimd.tensor_tensor(x1[:, 1, k, :], xres[:, k, :], f(x1[:, 0, k, :]),
                                            ALU.subtract).then_inc(s_x1lo, 1)
                for n in range(I_TILES):
                    pool.wait_ge(s_hhi, i * I_TILES + n + 1)
                    nc.gpsimd.tensor_tensor(hid(n, 1), slots[:, U_SLOT[n % 4], :], f(hid(n, 0)),
                                            ALU.subtract).then_inc(s_hlo, 1)

        @block.vector
        def _(dve):
            dve.wait_ge(s_const, 16 * 7)
            nc.vector.tensor_scalar(scale[:, :], scale[:, :], Q_STEP, None, ALU.mult).then_inc(s_init, 1)
            nc.vector.tensor_copy(eyeb[:, :], eyef[:, :]).then_inc(s_init, 1)
            nc.vector.tensor_reduce(headrow[:, :], eyef[0:NH, 0:NH].rearrange("h (g j) -> h g j", j=GROUPS),
                                    AX_X, ALU.max).then_inc(s_headrow, 1)
            dve.wait_ge(s_headrow, 1)
            nc.vector.tensor_copy(headsel[:, :, :], headrow[:, :].rearrange("h (g o) -> h g o", o=1)
                                  .broadcast_to([NH, NKV, P])).then_inc(s_init, 1)

            def resident_lo(r):
                sub = nc.vector.tensor_tensor
                dve.wait_ge(s_reshi, (1, 3, 7, 8)[r])
                if r == 3:
                    sub(guA[:, :, :, 2, :], raw_guA[:, :, :, 2, :], f(guA[:, :, :, 0, :]),
                        ALU.subtract).then_inc(s_reslo, 1)
                    return
                sub(guB[96:128, r - 1, :], raw_B[96:128], f(guB[96:128, r - 1, :]), ALU.subtract).then_inc(s_reslo, 1)
                if r == 1:
                    sub(dnB[96:128, :], raw_dB[96:128], f(dnB[96:128, :]), ALU.subtract).then_inc(s_reslo, 1)
                else:
                    sub(dnA[:, :, 2, :], raw_dA, f(dnA[:, :, 0, :]), ALU.subtract).then_inc(s_reslo, 1)

            def project_lo(k):
                dve.wait_ge(s_projhi, k + 1)
                nc.vector.tensor_tensor(projw[:, 1, k, :], raw_proj[:, k, :], f(projw[:, 0, k, :]),
                                        ALU.subtract).then_inc(s_projlo, 1)

            for i in range(HALVES):
                if i == 0:
                    project_lo(0)
                for k in range(KB):
                    dve.wait_ge(s_xchi, i * KB + k + 1)
                    nc.vector.tensor_tensor(xc[:, 1, k, :], bank[k][:, :], f(xc[:, 0, k, :]),
                                            ALU.subtract).then_inc(s_xclo, 1)
                if i == 0:
                    for k in range(1, KB):
                        project_lo(k)

                def rotate(t):
                    ps = bank[PROJ_BANK[t]]
                    dve.wait_ge(s_proj, i * PROJ + t + 1)
                    if t == 2:
                        dve.wait_ge(s_krope, i + 1)
                    if t >= 3:
                        dve.wait_ge(s_rope, i * GROUPS + t - 2)
                    nc.vector.stream_shuffle(slots[:, t % 2, :], ps[:, :],
                                             [16 * (p // 16) + (p + 8) % 16 for p in range(32)]).then_inc(s_sw, 1)
                    cos = rope[:, 0:1, :].broadcast_to([P, NB, S])
                    nc.vector.tensor_tensor(slots[:, R_SLOT[t], :].rearrange("p (b n) -> p b n", b=NB),
                                            ps[:, :].rearrange("p (b n) -> p b n", b=NB), cos,
                                            ALU.mult).then_inc(s_cos, 1)

                def rotate_k():
                    x, sw = slots[:, R_SLOT[0], :], slots[:, 0, :]
                    sw3 = sw.rearrange("p (b n) -> p b n", b=NB)
                    dve.wait_ge(s_sw, i * ROT + 1)
                    nc.vector.tensor_tensor(sw3, sw3, rope[:, 1:2, :].broadcast_to([P, NB, S]),
                                            ALU.mult).then_inc(s_ksin, 1)
                    dve.wait_ge(s_ksin, i + 1)
                    dve.wait_ge(s_cos, i * ROT + 1)
                    nc.vector.tensor_tensor(x, x, sw, ALU.add).then_inc(s_krope, 1)

                def k_lo(t):
                    dve.wait_ge(s_khi, i * 2 + t + 1)
                    nc.vector.tensor_tensor(kdup[t][64:128, :], kdup[t][64:128, :], f(khi[64:128, t, :]),
                                            ALU.subtract).then_inc(s_klo, 1)

                def q_lo(j):
                    dve.wait_ge(s_qhi, i * 16 + 4 * j + 3)
                    for t in range(2):
                        nc.vector.tensor_tensor(qlm[t][0:64, j, :], slots[64 * t:64 * t + 64, 4 + j, :],
                                                f(qhh[64 * t:64 * t + 64, t, j, :]), ALU.subtract).then_inc(s_qlo, 1)

                def maxima(s):
                    b, j, t = s // 8, s % 8 // 2, s % 2
                    at = S_BANK[ORDER.index(("scores", s)) % 3]
                    dve.wait_ge(s_S, i * 32 + s + 1)
                    nc.vector.tensor_reduce(mx[:, b % 2, 4 * t:4 * t + 4, j],
                                            bank[at][:, :].rearrange("p (g k) -> p g k", g=4),
                                            AX_X, ALU.max).then_inc(s_max, 1)

                def store_shift(b):
                    dve.wait_ge(s_mT, i * NB + b + 1)
                    at = S_BANK[ORDER.index(("max", b)) % 3]
                    mt = bank[at][0:NH, 0:S].rearrange("h (o q) -> h o q", o=1).broadcast_to([NH, GROUPS, S])
                    sel = headcol[:, :].rearrange("h (j o) -> h j o", o=1).broadcast_to([NH, GROUPS, S])
                    nc.vector.tensor_tensor(qlm[0][64:64 + NH, :, S * b:S * b + S], mt, sel,
                                            ALU.mult).then_inc(s_shift, 1)

                def reciprocal(b, j):
                    if j == 0:
                        dve.wait_ge(s_pused, i * 8 + 2 * b + 2)
                        if b >= 2:
                            dve.wait_ge(s_alo, i * ON + b - 1)
                    nc.vector.reciprocal(nrm[:, b % 2, S * j:S * j + S], bank[1 + b % 2][:, S * j:S * j + S]).then_inc(s_rec, 1)

                if i:
                    dve.wait_ge(s_out[i - 1], KB * 16)
                rotate(0)
                rotate_k()
                rotate(1)
                rotate(2)
                k_lo(0)
                k_lo(1)
                rotate(3)
                rotate(4)
                def read(n):
                    kind, at = ORDER[n]
                    (maxima if kind == "scores" else store_shift)(at)

                q_lo(0)
                read(0)
                read(1)
                q_lo(1)
                read(2)
                read(3)
                q_lo(2)
                for n in range(4, 8):
                    read(n)
                q_lo(3)
                for n in range(8, FIRST):
                    read(n)
                dve.wait_ge(s_vtr, i + 1)
                vt = bank[1][:, :].rearrange("p (b m c d) -> p b m c d", b=NB, m=PAIRS, c=2)
                vp = vpad[:, :, :, :].rearrange("p b (m c) n -> p b m c n", c=2)
                for c in range(2):
                    nc.vector.tensor_copy(vp[:, :, :, c, 16 * c:16 * c + 16], vt[:, :, :, c, :]).then_inc(s_v, 1)
                todo = [(b, j) for b in range(NB - 1) for j in range(GROUPS)]
                for n in range(FIRST, len(ORDER)):
                    read(n)
                    if n in RECIPROCALS_AT:
                        reciprocal(*todo.pop(0))
                for b, j in todo:
                    reciprocal(b, j)
                b = NB - 1
                for j in range(GROUPS):
                    reciprocal(b, j)
                    dve.wait_ge(s_rec, i * 16 + 4 * b + j + 1)
                    nc.vector.tensor_tensor(nrm[:, b % 2, S * j:S * j + S], bank[0][:, S * j:S * j + S],
                                            nrm[:, b % 2, S * j:S * j + S], ALU.mult).then_inc(s_onlast, 1)
                if i == 0:
                    resident_lo(1)
                for k in range(KB):
                    dve.wait_ge(s_wo, i * KB + k + 1)
                    nc.vector.tensor_tensor(xres[:, k, :], bank[4 + k][:, :], xres[:, k, :],
                                            ALU.add).then_inc(s_x1, 1)
                if i == 0:
                    resident_lo(2)
                dve.wait_ge(s_lbhi, i + 1)
                nc.vector.scalar_tensor_tensor(out=loraBp[:, 1, :], in0=loraB[:, :], scalar=LORA_SCALE,
                                               in1=f(loraBp[:, 0, :]), op0=ALU.mult,
                                               op1=ALU.subtract).then_inc(s_lblo, 1)
                if i == 0:
                    dve.wait_ge(s_lzero, 1)
                for b in range(NB):
                    dve.wait_ge(s_lh, i * NB + b + 1)
                    block_b = lorah[32 * b:32 * b + 32, S * b:S * b + S]
                    turned = bank[4][32 * b:32 * b + 32, 0:S]
                    nc.vector.tensor_copy(block_b, turned).then_inc(s_lhhi, 1)
                    dve.wait_ge(s_lhhi, i * NB + b + 1)
                    nc.vector.scalar_tensor_tensor(out=block_b, in0=f(block_b), scalar=keyrow[32 * b:32 * b + 32, 4:5],
                                                   in1=turned, op0=ALU.mult, op1=ALU.add).then_inc(s_lhs, 1)
                if i == 0:
                    resident_lo(3)
                for k in range(KB):
                    dve.wait_ge(s_xbhi, i * KB + k + 1)
                    nc.vector.scalar_tensor_tensor(out=xb[:, 1, k, :], in0=bank[k][:, :], scalar=bias2[:, k:k + 1],
                                                   in1=f(xb[:, 0, k, :]), op0=ALU.add,
                                                   op1=ALU.subtract).then_inc(s_xblo, 1)

                def low_rank(k, w, ps):
                    dve.wait_ge(s_zp, i * 3 + k + 1)
                    nc.vector.tensor_copy(z[:, w, :], ps[:, :]).then_inc(s_zhi, 1)
                    dve.wait_ge(s_zhi, i * 3 + k + 1)
                    nc.vector.tensor_tensor(z[R:2 * R, w, :], ps[R:2 * R, :], f(z[R:2 * R, w, :]),
                                            ALU.subtract).then_inc(s_z, 1)

                def convert(m):
                    wait_convert(dve, i, m)
                    nc.vector.tensor_scalar(wf[:, m % 2, 0:512], stage[:, wi(m), 0:512].bitcast(I32), -Q_ZERO, None,
                                            ALU.add).then_inc(s_wf, 1)

                def hidden(n):
                    g, u, th = slots[:, n % 2, :], slots[:, U_SLOT[n % 4], :], slots[:, 4 + n % 2, :]
                    dve.wait_ge(s_th, i * I_TILES + n + 1)
                    nc.vector.scalar_tensor_tensor(out=th, in0=th, scalar=1.0, in1=g, op0=ALU.add,
                                                   op1=ALU.mult).then_inc(s_h1, 1)
                    dve.wait_ge(s_h1, i * I_TILES + n + 1)
                    dve.wait_ge(s_u, i * I_TILES + n + 1)
                    nc.vector.scalar_tensor_tensor(out=u, in0=th, scalar=0.5, in1=u, op0=ALU.mult,
                                                   op1=ALU.mult).then_inc(s_h, 1)

                convert(0)
                convert(1)
                low_rank(0, 0, bank[5])
                low_rank(1, 1, bank[6])
                for n in range(I_TILES):
                    gl, ul = bank[4 * (n % 2) + 2], bank[4 * (n % 2) + 3]
                    g, u = slots[:, n % 2, :], slots[:, U_SLOT[n % 4], :]
                    convert(n + 2)
                    dve.wait_ge(s_tgu, i * 2 * I_TILES + 2 * n + 1)
                    nc.vector.scalar_tensor_tensor(out=g, in0=gl[:, :], scalar=LR_SCALE, in1=g, op0=ALU.mult,
                                                   op1=ALU.add).then_inc(s_g, 1)
                    dve.wait_ge(s_tgu, i * 2 * I_TILES + 2 * n + 2)
                    nc.vector.scalar_tensor_tensor(out=u, in0=ul[:, :], scalar=LR_SCALE, in1=u, op0=ALU.mult,
                                                   op1=ALU.add).then_inc(s_u, 1)
                    if n:
                        hidden(n - 1)
                hidden(I_TILES - 1)
                for m in range(I_TILES + 2, LATE + I_TILES + 1):
                    convert(m)
                low_rank(2, 0, bank[0])
                for m in range(LATE + I_TILES + 1, W_CHUNKS):
                    convert(m)
                for k in range(KB):
                    dve.wait_ge(s_dl, i * KB + k + 1)
                    nc.vector.scalar_tensor_tensor(out=slots[:, k, :], in0=bank[k][:, :], scalar=LR_SCALE,
                                                   in1=xres[:, k, :], op0=ALU.mult, op1=ALU.add).then_inc(s_t, 1)
                for k in range(KB):
                    dve.wait_ge(s_t, i * KB + k + 1)
                    dve.wait_ge(s_dno, i * KB + k + 1)
                    nc.vector.scalar_tensor_tensor(out=slots[:, k, :], in0=bank[4 + k][:, :],
                                                   scalar=scale[:, 2 * I_TILES + k:2 * I_TILES + k + 1],
                                                   in1=slots[:, k, :], op0=ALU.mult, op1=ALU.add).then_inc(s_y, 1)

        @block.tensor
        def _(pe):
            mm = nc.tensor.matmul

            def split3(ps, whi, wlo, xhi, xlo, start, stop):
                mm(ps, whi, xhi, start=start, stop=False)
                mm(ps, whi, xlo, start=False, stop=False)
                return mm(ps, wlo, xhi, start=False, stop=stop)

            def keep_warm(n, k):
                for _ in range(n):
                    mm(bank[k][:, :], eyeb[:, :], maskq[:, :], start=True, stop=True)

            pe.wait_ge(s_init, 3)
            keep_warm(WARM[0], 0)
            for i in range(HALVES):
                if i:
                    pe.wait_ge(s_t, i * KB)
                    keep_warm(WARM[1], 0)
                for b in range(NB):
                    pe.wait_ge(s_x[b], i * 16 + 16)
                    pe.wait_ge(s_wc[b], i * 16 + 16)
                    w = adapter[i][b].rearrange("p (k n) -> p k n", k=KB)
                    for o in range(KB):
                        for k in range(KB):
                            last = mm(bank[o][:, S * b:S * b + S], w[:, k, P * o:P * o + P],
                                      xres[:, k, S * b:S * b + S], start=(k == 0), stop=(k == KB - 1))
                        if b == NB - 1:
                            last.then_inc(s_cond, 1)
                    if b < NB - 1:
                        last.then_inc(s_condb, 1)

                def project(t, k):
                    last = split3(bank[PROJ_BANK[t]][:, :], projw[:, 0, k, P * t:P * t + P],
                                  projw[:, 1, k, P * t:P * t + P], xc[:, 0, k, :], xc[:, 1, k, :],
                                  k == 0, k == KB - 1)
                    if k == KB - 1:
                        last.then_inc(s_proj, 1)

                if i:
                    pe.wait_ge(s_y, i * KB)
                for k in range(KB):
                    pe.wait_ge(s_xclo, i * KB + k + 1)
                    if i == 0:
                        pe.wait_ge(s_projlo, k + 1)
                    for t in range(2):
                        project(t, k)

                def bank_read(n):
                    if n >= 3:
                        kind, at = ORDER[n - 3]
                        if kind == "scores":
                            pe.wait_ge(s_max, i * 32 + at + 1)
                        else:
                            pe.wait_ge(s_shift, i * NB + at + 1)
                    elif n == 0:
                        pe.wait_ge(s_cos, i * ROT + 2)

                def scores(s):
                    b, j, t = s // 8, s % 8 // 2, s % 2
                    n = ORDER.index(("scores", s))
                    ps = bank[S_BANK[n % 3]]
                    if b == 0:
                        pe.wait_ge(s_km, i * 8 + 4 * t + 4)
                        pe.wait_ge(s_qhi, i * 16 + 4 * j + 2 * t + 2)
                    bank_read(n)
                    mm(ps[:, :], eyeb[:, :], maskq[:, :], start=True, stop=False)
                    mm(ps[:, :], qhh[:, t, j, S * b:S * b + S], khl[:, 4 * t:4 * t + 4, S * b:S * b + S],
                       start=False, stop=True).then_inc(s_S, 1)

                def turn_max(b):
                    n = ORDER.index(("max", b))
                    bank_read(n)
                    pe.wait_ge(s_max, i * 32 + 8 * b + 8)
                    nc.tensor.transpose(bank[S_BANK[n % 3]][0:NH, 0:S],
                                        mx[:, b % 2, :, :].rearrange("p g j -> p (g j)"),
                                        eyef[:, :]).then_inc(s_mT, 1)

                def scores_turned(s):
                    b, g = s // 8, ST_ORDER[s % 8]
                    ps = bank[ST_BANK[s % 2]]
                    if b == 0:
                        pe.wait_ge(s_ksel[g // 4], i * 16 + 16)
                        pe.wait_ge(s_sel, (i + 1) * 16 * NB)
                        pe.wait_ge(s_qlo, i * 8 + 8)
                    if s % 8 == 0:
                        pe.wait_ge(s_shift, i * NB + b + 1)
                    if g // 4 and ST_ORDER.index(4) == s % 8:
                        pe.wait_ge(s_shift2, i * NB + b + 1)
                    if s >= 2:
                        pe.wait_ge(s_exp, i * 32 + s - 1)
                    tokens = slice(S * b, S * b + S)
                    mm(ps[:, :], khl[:, g, tokens], qhh[:, g // 4, :, tokens], start=True, stop=False)
                    mm(ps[:, :], ksel[0:64 + NH, g, tokens], qlm[g // 4][0:64 + NH, :, tokens],
                       start=False, stop=True).then_inc(s_ST, 1)

                def values(b, c):
                    if b == 0:
                        pe.wait_ge(s_v, i * 2 + 2)
                    if c == 0 and b:
                        pe.wait_ge(s_pv, i * (NB - 1) + b)
                    if c == 0 and b > 1:
                        pe.wait_ge(s_rec, i * 16 + 4 * b - 4)
                    pe.wait_ge(s_p, i * 32 + 8 * b + 4 * c + 4)
                    for m in range(PAIRS):
                        mm(bank[0][32 * m:32 * m + 32, :], vpad[:, b, 2 * m + c, :], slots[:, 4 * c + m, :],
                           start=(c == 0), stop=(c == 1), tile_position=(0, 32 * m))
                    for m in range(PAIRS):
                        last = mm(bank[1 + b % 2][32 * m:32 * m + 32, :], ones2[:, c, :], slots[:, 4 * c + m, :],
                                  start=(c == 0), stop=(c == 1), tile_position=(0, 32 * m))
                    last.then_inc(s_pused, 1)

                for t in range(2, PROJ):
                    for k in range(KB):
                        project(t, k)
                keep_warm(WARM[2], 1)
                for s in range(6):
                    scores(s)
                    if s % 2:
                        keep_warm(WARM[3], 1)
                pe.wait_ge(s_zeros, 4)
                pe.wait_ge(s_vT, i + 1)
                for b in range(NB):
                    last = nc.tensor.transpose(bank[1][:, S * b:S * b + S], nrm[:, 0, S * b:S * b + S], eyef[:, :])
                last.then_inc(s_vtr, 1)
                scores(6)
                scores(7)
                keep_warm(WARM[4], 0)
                def issue(n):
                    kind, at = ORDER[n]
                    (scores if kind == "scores" else turn_max)(at)

                for n in range(8, FIRST):
                    issue(n)
                issued = FIRST
                for s in range(8 * NB):
                    b, n = s // 8, s % 8
                    scores_turned(s)
                    while issued < min(LEAD + s + 1 + s // 8, len(ORDER)):
                        issue(issued)
                        issued += 1
                    for c in range(2):
                        if b and n == VALUES_AT[c]:
                            values(b - 1, c)
                for c in range(2):
                    values(NB - 1, c)

                keep_warm(WARM[5], 3)
                if i == 0:
                    pe.wait_ge(s_wolo, 1)
                for j in range(GROUPS):
                    pe.wait_ge(s_alo, i * ON + NB + j)
                    for o in range(KB):
                        last = split3(bank[4 + o][:, :], wow[:, 0, j, P * o:P * o + P], wow[:, 1, j, P * o:P * o + P],
                                      att[:, 0, j, :], att[:, 1, j, :], j == 0, j == GROUPS - 1)
                        if j == GROUPS - 1:
                            last.then_inc(s_wo, 1)
                for k in range(KB):
                    pe.wait_ge(s_w2lo, i * KB + k + 1)
                    pe.wait_ge(s_x1lo, i * KB + k + 1)
                    if k == KB - 1:
                        pe.wait_ge(s_la, (i + 1) * 16 * NB)
                        for b in range(NB):
                            for kk in range(KB):
                                last = mm(bank[4][32 * b:32 * b + 32, 0:S], loraA[:, b, kk, :],
                                          xres[:, kk, S * b:S * b + S], start=(kk == 0), stop=(kk == KB - 1),
                                          tile_position=(0, 32 * b))
                            last.then_inc(s_lh, 1)
                    for o in range(KB):
                        split3(bank[o][:, :], w2[:, 0, k, P * o:P * o + P], w2[:, 1, k, P * o:P * o + P],
                               x1[:, 0, k, :], x1[:, 1, k, :], k == 0, False)
                pe.wait_ge(s_lblo, i + 1)
                pe.wait_ge(s_lhs, i * NB + NB)
                for o in range(KB):
                    mm(bank[o][:, :], loraBp[:, 0, P * o:P * o + P], lorah[:, :], start=False, stop=False)
                    mm(bank[o][:, :], loraBp[:, 1, P * o:P * o + P], lorah[:, :], start=False,
                       stop=True).then_inc(s_c2, 1)
                if i == 0:
                    pe.wait_ge(s_reslo, 5)
                for k in range(KB):
                    pe.wait_ge(s_xblo, i * KB + k + 1)
                    for w in range(2):
                        wt = guA[:, w, k, :, :].rearrange("p c r -> p (c r)")
                        mm(bank[5 + w][:, :], wt, xb[:, 0, k, :], start=(k == 0), stop=False)
                        last = mm(bank[5 + w][:, :], wt, xb[:, 1, k, :], start=False, stop=(k == KB - 1))
                        if k == KB - 1:
                            last.then_inc(s_zp, 1)
                for n in range(I_TILES):
                    ps = [bank[4 * (n % 2) + c] for c in range(4)]
                    if n >= 2:
                        pe.wait_ge(s_u, i * I_TILES + n - 1)
                    pe.wait_ge(s_wf, i * W_CHUNKS + n + 1)
                    pe.wait_ge(s_wfu, i * U_CHUNKS + n + 1)
                    wt = wf[:, n % 2, :].rearrange("p (w k o) -> p w k o", w=2, k=KB)
                    for w in range(2):
                        for k in range(KB):
                            mm(ps[w][:, :], wt[:, w, k, :], xb[:, 0, k, :], start=(k == 0), stop=False)
                            mm(ps[w][:, :], wt[:, w, k, :], xb[:, 1, k, :], start=False, stop=(k == KB - 1))
                    if n == 0:
                        pe.wait_ge(s_z, i * 3 + 2)
                    for w in range(2):
                        last = mm(ps[2 + w][:, :], guB[:, w, P * n:P * n + P], z[:, w, :], start=True, stop=True)
                    last.then_inc(s_gu, 1)
                pe.wait_ge(s_u, i * I_TILES + I_TILES - 1)
                for c in range(D_CHUNKS):
                    m = I_TILES + c
                    if c == LATE:
                        pe.wait_ge(s_hlo, (i + 1) * I_TILES)
                        for n in range(I_TILES):
                            wt = dnA[:, n, :, :].rearrange("p c r -> p (c r)")
                            mm(bank[0][:, :], wt, hid(n, 0), start=(n == 0), stop=False)
                            last = mm(bank[0][:, :], wt, hid(n, 1), start=False, stop=(n == I_TILES - 1))
                        last.then_inc(s_zp, 1)
                    if c == LATE + 1:
                        pe.wait_ge(s_z, i * 3 + 3)
                        for o in range(KB):
                            mm(bank[o][:, :], dnB[:, P * o:P * o + P], z[:, 0, :], start=True,
                               stop=True).then_inc(s_dl, 1)
                    pe.wait_ge(s_wf, i * W_CHUNKS + m + 1)
                    pe.wait_ge(s_wfu, i * U_CHUNKS + min(m + 1, U_CHUNKS))
                    for n in range(2 * c, min(2 * c + 2, I_TILES)):
                        pe.wait_ge(s_hlo, i * I_TILES + n + 1)
                        for o in range(KB):
                            wt = wf[:, m % 2, 512 * (n % 2) + P * o:512 * (n % 2) + P * o + P]
                            mm(bank[4 + o][:, :], wt, hid(n, 0), start=(n == 0), stop=False)
                            last = mm(bank[4 + o][:, :], wt, hid(n, 1), start=False, stop=(n == I_TILES - 1))
                            if n == I_TILES - 1:
                                last.then_inc(s_dno, 1)
                    if c < D_CHUNKS - 1:
                        last.then_inc(s_dn, 1)


def kernel(**inputs):
    import numpy as np
    import ml_dtypes
    import concourse.bacc as bacc
    from concourse.bass_utils import run_bass_kernel_spmd

    a = {k: np.asarray(v) for k, v in inputs.items()}

    def blocks(w):
        return w.reshape(-1, P, w.shape[1]).transpose(1, 0, 2).reshape(P, -1)

    def pad(w, axis):
        n = IP - w.shape[axis]
        return np.pad(w, [(0, n if d == axis else 0) for d in range(w.ndim)])

    arrays = {}
    arrays["xT"] = a["x"].reshape(HALVES, T, KB, P).transpose(0, 3, 2, 1)
    arrays["ids"] = np.concatenate([a["itok_B_3_7"], a["itok_B_0_23"]]).reshape(1, 2 * B)
    arrays["cond_w"] = a["L0_cond_weight"].transpose(0, 2, 1).reshape(ADAPTERS, KB, P, H).transpose(
        0, 2, 1, 3).reshape(ADAPTERS, P, KB * H)
    wq = a["L0_attn_wq"].reshape(NKV, GROUPS, HD, H)
    rows = [a["L0_attn_wk"]]
    rows += [wq[:, j].reshape(P, H) for j in range(GROUPS)] + [a["L0_attn_wv"]]
    arrays["proj_w"] = blocks(np.concatenate(rows).T)
    wo = a["L0_attn_wo"].T.reshape(NKV, GROUPS, HD, H).transpose(1, 0, 2, 3).reshape(H, H)
    arrays["wo_w"] = blocks(wo)
    arrays["c2_w"] = blocks(a["L0_cond2_W"].T)
    arrays["c2_b"] = a["L0_cond2_b"].reshape(KB, P).T
    c2_A = np.tile(a["L0_cond2_lora_As"], (1, 1, 2))
    arrays["c2_A"] = c2_A.reshape(SLOTS, KB, P, 2 * R2).transpose(0, 2, 1, 3).reshape(SLOTS, P, KB * 2 * R2)
    arrays["c2_B"] = np.tile(a["L0_cond2_lora_Bs"], (1, 2, 1))
    gu = np.stack([pad(a[f"L0_ffn_{n}_q"], 0) for n in ("gate", "up")])
    arrays["gu_q"] = gu.reshape(2, I_TILES, P, KB, P).transpose(1, 4, 0, 3, 2).reshape(I_TILES, P, 2 * KB * P)
    dn = pad(a["L0_ffn_down_q"].T, 0)
    dn = np.pad(dn, [(0, (2 * D_CHUNKS - I_TILES) * P), (0, 0)])
    arrays["dn_q"] = dn.reshape(D_CHUNKS, 2, P, H).transpose(0, 2, 1, 3).reshape(D_CHUNKS, P, 2 * H)
    arrays["scales"] = np.concatenate(
        [pad(a[f"L0_ffn_{n}_scale"], 0).reshape(I_TILES, P).T for n in ("gate", "up")]
        + [a["L0_ffn_down_scale"].reshape(KB, P).T], axis=1)
    arrays["gA"] = blocks(np.tile(a["L0_ffn_gate_A"], (1, 4)))
    arrays["uA"] = blocks(np.tile(a["L0_ffn_up_A"], (1, 4)))
    arrays["gB"] = np.tile(pad(a["L0_ffn_gate_B"], 1), (4, 1))
    arrays["uB"] = np.tile(pad(a["L0_ffn_up_B"], 1), (4, 1))
    arrays["dA"] = blocks(pad(a["L0_ffn_down_A"], 0))
    arrays["dB"] = np.tile(a["L0_ffn_down_B"], (4, 1))
    freq = (1.0 / np.float32(10000.0) ** (np.arange(0, HD, 2, dtype=np.float32) / np.float32(HD))).astype(np.float32)
    angle = np.arange(S, dtype=np.float32)[None, :] * np.concatenate([freq, freq])[:, None]
    sign = np.where(np.arange(HD) < HD // 2, -1.0, 1.0).astype(np.float32)[:, None]
    arrays["rope_tab"] = np.tile(np.stack([np.cos(angle), np.sin(angle) * sign], 1), (P // HD, 1, 1)).astype(np.float32)
    q, k = np.arange(S)[:, None], np.arange(S)[None, :]
    arrays["causal"] = np.tile(np.where(k <= q, 0.0, MASKED), (1, NB)).astype(ml_dtypes.bfloat16)
    arrays["eye"] = np.eye(P, dtype=np.float32)
    rows = np.arange(P)[:, None]
    arrays["key_rows"] = np.concatenate([rows % 64 // HD == np.arange(4), rows % 32 >= R2], axis=1) * np.float32(
        [1, 1, 1, 1, -1])
    arrays["head_cols"] = -(np.arange(NH)[:, None] % GROUPS == np.arange(GROUPS)).astype(np.float32)

    nc = bacc.Bacc("TRN2", target_bir_lowering=False, num_devices=1)
    aps, ins = {}, {}
    for name, v in arrays.items():
        v = np.ascontiguousarray(v)
        ins[f"in_{name}_dram"] = v
        aps[name] = nc.dram_tensor(f"in_{name}_dram", v.shape, mybir.dt.from_np(v.dtype), kind="ExternalInput").ap()
    out = nc.dram_tensor("out_0_dram", (HALVES, P, KB, T), F32, kind="ExternalOutput").ap()
    adaln_attn_ffn(nc, out=out, **aps)
    r = run_bass_kernel_spmd(nc, [ins], core_ids=[0])
    got = r.results[0]["out_0_dram"]
    return np.ascontiguousarray(got.transpose(0, 3, 2, 1)).reshape(B, S, H)
```
